# Optimizing a Trainium2 kernel written in Bass

```python
import numpy as np
import jax
import jax.numpy as jnp

def _softmax(x, axis=-1):
    return jax.nn.softmax(x, axis=axis)

def _gelu(x):
    return jax.nn.gelu(x, approximate=True)

def _silu(x):
    return jax.nn.silu(x)

def _sigmoid(x):
    return jax.nn.sigmoid(x)

def _layernorm(x, axis=-1, eps=1e-05):
    m = jnp.mean(x, axis=axis, keepdims=True)
    v = jnp.var(x, axis=axis, keepdims=True)
    return (x - m) / jnp.sqrt(v + eps)

def _scatter_add(tgt, idx, src, axis=0):
    return tgt.at[idx].add(src)

def _segment_sum(src, seg, n):
    return jax.ops.segment_sum(src, seg, n)
kernel_name = 'mk_sandwich_d1_jaxref_r8_809da3'

def setup_inputs(seed: int=0):
    np.random.seed(seed)
    _w = jnp.asarray

    def _L0_attn_setup():
        import jax, jax.numpy as jnp
        import numpy as np
        B, S, H = (4, 512, 128)
        GAMMA = 0.96875

        def decay_mask(seq_len, gamma, dtype=jnp.float32):
            i = jnp.arange(seq_len)[:, None]
            j = jnp.arange(seq_len)[None, :]
            exp = (i - j).astype(dtype)
            return jnp.where(i >= j, jnp.power(jnp.asarray(gamma, dtype), exp), jnp.zeros((), dtype))
        key = jax.random.key(seed)
        ks = jax.random.split(key, 6)
        sc = 1.0 / np.sqrt(H)
        return {'x': jax.random.normal(ks[0], (B, S, H), dtype=jnp.float32), 'Wq': jax.random.normal(ks[1], (H, H), dtype=jnp.float32) * sc, 'bq': jax.random.normal(ks[2], (H,), dtype=jnp.float32) * 0.01, 'Wk': jax.random.normal(ks[3], (H, H), dtype=jnp.float32) * sc, 'bk': jax.random.normal(ks[4], (H,), dtype=jnp.float32) * 0.01, 'Wv': jax.random.normal(ks[5], (H, H), dtype=jnp.float32) * sc}
    _L0_attn_in = _L0_attn_setup()

    def _L0_ffn_setup():
        import jax, jax.numpy as jnp
        import numpy as np
        DIM = 128
        DEPTH = 2
        HEADS = 8
        DIM_HEAD = 64
        WINDOW = 64
        INNER = HEADS * DIM_HEAD
        HID = int(DIM * 4 * 2 / 3)
        B, N = (2, 1024)
        QK_SCALE = 8.0

        def shift_token(t):
            t1, t2 = jnp.split(t, 2, axis=-1)
            t2 = jnp.pad(t2, ((0, 0), (1, 0), (0, 0)))[:, :-1]
            return jnp.concatenate([t1, t2], axis=-1)

        def l2norm(t):
            return t / jnp.clip(jnp.linalg.norm(t, axis=-1, keepdims=True), 1e-12)

        def rotate_half(x):
            x1, x2 = jnp.split(x, 2, axis=-1)
            return jnp.concatenate([-x2, x1], axis=-1)

        def rotary_xpos(q, k):
            n = q.shape[-2]
            half_idx = jnp.arange(0, DIM_HEAD, 2, dtype=jnp.float32)
            inv_freq = 1.0 / 10000.0 ** (half_idx / DIM_HEAD)
            t = jnp.arange(n, dtype=jnp.float32)
            freqs = t[:, None] * inv_freq[None, :]
            freqs = jnp.concatenate([freqs, freqs], axis=-1)
            base = (half_idx + 0.4 * DIM_HEAD) / (1.4 * DIM_HEAD)
            power = (t - n // 2) / float(WINDOW // 2)
            scale = base[None, :] ** power[:, None]
            scale = jnp.concatenate([scale, scale], axis=-1)
            cos, sin = (jnp.cos(freqs), jnp.sin(freqs))
            q = q * cos * scale + rotate_half(q) * sin * scale
            k = k * cos / scale + rotate_half(k) * sin / scale
            return (q, k)

        def local_attention(q, k, v):
            b, h, n, d = q.shape
            w = n // WINDOW
            bq = q.reshape(b, h, w, WINDOW, d) * QK_SCALE
            bk = k.reshape(b, h, w, WINDOW, d)
            bv = v.reshape(b, h, w, WINDOW, d)

            def look_around(t):
                p = jnp.pad(t, ((0, 0), (0, 0), (1, 0), (0, 0), (0, 0)))
                return jnp.concatenate([p[:, :, :w], p[:, :, 1:]], axis=3)
            bk, bv = (look_around(bk), look_around(bv))
            bt = jnp.arange(n).reshape(w, WINDOW)
            btp = jnp.pad(bt, ((1, 0), (0, 0)), constant_values=-1)
            btk = jnp.concatenate([btp[:w], btp[1:]], axis=1)
            sim = jnp.einsum('bhwid,bhwjd->bhwij', bq, bk)
            i = bt[:, :, None]
            j = btk[:, None, :]
            mask = (i < j) | (i > j + WINDOW) | (j == -1)
            sim = jnp.where(mask, -jnp.finfo(sim.dtype).max, sim)
            attn = jax.nn.softmax(sim, axis=-1)
            out = jnp.einsum('bhwij,bhwjd->bhwid', attn, bv)
            return out.reshape(b, h, n, d)

        def _layer(x, wqkv, qs, ksc, wo, lg, lb, w1, b1, w2, b2):
            b, n, _ = x.shape
            h = shift_token(x)
            qkv = h @ wqkv
            q, k, v = jnp.split(qkv, 3, axis=-1)
            to_heads = lambda t: t.reshape(b, n, HEADS, DIM_HEAD).transpose(0, 2, 1, 3)
            q, k, v = (to_heads(q), to_heads(k), to_heads(v))
            q = l2norm(q) * qs
            k = l2norm(k) * ksc
            q, k = rotary_xpos(q, k)
            o = local_attention(q, k, v)
            o = o.transpose(0, 2, 1, 3).reshape(b, n, INNER)
            x = x + o @ wo
            h = shift_token(x)
            mu = h.mean(-1, keepdims=True)
            var = h.var(-1, keepdims=True)
            h = (h - mu) / jnp.sqrt(var + 1e-05) * lg + lb
            h = h @ w1 + b1
            a, g = jnp.split(h, 2, axis=-1)
            h = a * jax.nn.gelu(g, approximate=False)
            x = x + h @ w2 + b2
            return x
        key = jax.random.key(seed)
        ks = jax.random.split(key, 6)
        return {'x': jax.random.normal(ks[0], (B, N, DIM), jnp.float32), 'wqkv': jax.random.normal(ks[1], (DEPTH, DIM, 3 * INNER), jnp.float32) * 0.02, 'q_scale': jnp.ones((DEPTH, DIM_HEAD), jnp.float32), 'k_scale': jnp.ones((DEPTH, DIM_HEAD), jnp.float32), 'wo': jax.random.normal(ks[2], (DEPTH, INNER, DIM), jnp.float32) * 0.02, 'ln_g': jnp.ones((DEPTH, DIM), jnp.float32), 'ln_b': jnp.zeros((DEPTH, DIM), jnp.float32), 'w1': jax.random.normal(ks[3], (DEPTH, DIM, 2 * HID), jnp.float32) * 0.02, 'b1': jnp.zeros((DEPTH, 2 * HID), jnp.float32), 'w2': jax.random.normal(ks[4], (DEPTH, HID, DIM), jnp.float32) * 0.02, 'b2': jnp.zeros((DEPTH, DIM), jnp.float32)}
    _L0_ffn_in = _L0_ffn_setup()
    _d = {'L0_attn_x': _L0_attn_in['x'], 'L0_attn_Wq': _L0_attn_in['Wq'], 'L0_attn_bq': _L0_attn_in['bq'], 'L0_attn_Wk': _L0_attn_in['Wk'], 'L0_attn_bk': _L0_attn_in['bk'], 'L0_attn_Wv': _L0_attn_in['Wv'], 'L0_ffn_wqkv': _L0_ffn_in['wqkv'], 'L0_ffn_q_scale': _L0_ffn_in['q_scale'], 'L0_ffn_k_scale': _L0_ffn_in['k_scale'], 'L0_ffn_wo': _L0_ffn_in['wo'], 'L0_ffn_ln_g': _L0_ffn_in['ln_g'], 'L0_ffn_ln_b': _L0_ffn_in['ln_b'], 'L0_ffn_w1': _L0_ffn_in['w1'], 'L0_ffn_b1': _L0_ffn_in['b1'], 'L0_ffn_w2': _L0_ffn_in['w2'], 'L0_ffn_b2': _L0_ffn_in['b2']}
    _x0 = _d['L0_attn_x']
    _d['L0_attn_x'] = jax.random.normal(jax.random.fold_in(jax.random.key(seed), 1), (16, 512, 128), dtype=_x0.dtype)
    del _x0
    return _d

def reference(L0_attn_x, L0_attn_Wq, L0_attn_bq, L0_attn_Wk, L0_attn_bk, L0_attn_Wv, L0_ffn_wqkv, L0_ffn_q_scale, L0_ffn_k_scale, L0_ffn_wo, L0_ffn_ln_g, L0_ffn_ln_b, L0_ffn_w1, L0_ffn_b1, L0_ffn_w2, L0_ffn_b2):

    def _L0_attn_ref(x, Wq, bq, Wk, bk, Wv):
        import jax, jax.numpy as jnp
        import numpy as np
        B, S, H = (4, 512, 128)
        GAMMA = 0.96875

        def decay_mask(seq_len, gamma, dtype=jnp.float32):
            i = jnp.arange(seq_len)[:, None]
            j = jnp.arange(seq_len)[None, :]
            exp = (i - j).astype(dtype)
            return jnp.where(i >= j, jnp.power(jnp.asarray(gamma, dtype), exp), jnp.zeros((), dtype))
        seq_len = x.shape[1]
        q = jnp.einsum('bsh,oh->bso', x, Wq) + bq
        k = jnp.einsum('bsh,oh->bso', x, Wk) + bk
        v = jnp.einsum('bsh,oh->bso', x, Wv)
        D = decay_mask(seq_len, GAMMA, x.dtype)
        scores = jnp.einsum('bqh,bkh->bqk', q, k) * D[None]
        return jnp.einsum('bqk,bkh->bqh', scores, v)

    def _L0_ffn_ref(x, wqkv, q_scale, k_scale, wo, ln_g, ln_b, w1, b1, w2, b2):
        import jax, jax.numpy as jnp
        import numpy as np
        DIM = 128
        DEPTH = 2
        HEADS = 8
        DIM_HEAD = 64
        WINDOW = 64
        INNER = HEADS * DIM_HEAD
        HID = int(DIM * 4 * 2 / 3)
        B, N = (2, 1024)
        QK_SCALE = 8.0

        def shift_token(t):
            t1, t2 = jnp.split(t, 2, axis=-1)
            t2 = jnp.pad(t2, ((0, 0), (1, 0), (0, 0)))[:, :-1]
            return jnp.concatenate([t1, t2], axis=-1)

        def l2norm(t):
            return t / jnp.clip(jnp.linalg.norm(t, axis=-1, keepdims=True), 1e-12)

        def rotate_half(x):
            x1, x2 = jnp.split(x, 2, axis=-1)
            return jnp.concatenate([-x2, x1], axis=-1)

        def rotary_xpos(q, k):
            n = q.shape[-2]
            half_idx = jnp.arange(0, DIM_HEAD, 2, dtype=jnp.float32)
            inv_freq = 1.0 / 10000.0 ** (half_idx / DIM_HEAD)
            t = jnp.arange(n, dtype=jnp.float32)
            freqs = t[:, None] * inv_freq[None, :]
            freqs = jnp.concatenate([freqs, freqs], axis=-1)
            base = (half_idx + 0.4 * DIM_HEAD) / (1.4 * DIM_HEAD)
            power = (t - n // 2) / float(WINDOW // 2)
            scale = base[None, :] ** power[:, None]
            scale = jnp.concatenate([scale, scale], axis=-1)
            cos, sin = (jnp.cos(freqs), jnp.sin(freqs))
            q = q * cos * scale + rotate_half(q) * sin * scale
            k = k * cos / scale + rotate_half(k) * sin / scale
            return (q, k)

        def local_attention(q, k, v):
            b, h, n, d = q.shape
            w = n // WINDOW
            bq = q.reshape(b, h, w, WINDOW, d) * QK_SCALE
            bk = k.reshape(b, h, w, WINDOW, d)
            bv = v.reshape(b, h, w, WINDOW, d)

            def look_around(t):
                p = jnp.pad(t, ((0, 0), (0, 0), (1, 0), (0, 0), (0, 0)))
                return jnp.concatenate([p[:, :, :w], p[:, :, 1:]], axis=3)
            bk, bv = (look_around(bk), look_around(bv))
            bt = jnp.arange(n).reshape(w, WINDOW)
            btp = jnp.pad(bt, ((1, 0), (0, 0)), constant_values=-1)
            btk = jnp.concatenate([btp[:w], btp[1:]], axis=1)
            sim = jnp.einsum('bhwid,bhwjd->bhwij', bq, bk)
            i = bt[:, :, None]
            j = btk[:, None, :]
            mask = (i < j) | (i > j + WINDOW) | (j == -1)
            sim = jnp.where(mask, -jnp.finfo(sim.dtype).max, sim)
            attn = jax.nn.softmax(sim, axis=-1)
            out = jnp.einsum('bhwij,bhwjd->bhwid', attn, bv)
            return out.reshape(b, h, n, d)

        def _layer(x, wqkv, qs, ksc, wo, lg, lb, w1, b1, w2, b2):
            b, n, _ = x.shape
            h = shift_token(x)
            qkv = h @ wqkv
            q, k, v = jnp.split(qkv, 3, axis=-1)
            to_heads = lambda t: t.reshape(b, n, HEADS, DIM_HEAD).transpose(0, 2, 1, 3)
            q, k, v = (to_heads(q), to_heads(k), to_heads(v))
            q = l2norm(q) * qs
            k = l2norm(k) * ksc
            q, k = rotary_xpos(q, k)
            o = local_attention(q, k, v)
            o = o.transpose(0, 2, 1, 3).reshape(b, n, INNER)
            x = x + o @ wo
            h = shift_token(x)
            mu = h.mean(-1, keepdims=True)
            var = h.var(-1, keepdims=True)
            h = (h - mu) / jnp.sqrt(var + 1e-05) * lg + lb
            h = h @ w1 + b1
            a, g = jnp.split(h, 2, axis=-1)
            h = a * jax.nn.gelu(g, approximate=False)
            x = x + h @ w2 + b2
            return x
        for l in range(DEPTH):
            x = _layer(x, wqkv[l], q_scale[l], k_scale[l], wo[l], ln_g[l], ln_b[l], w1[l], b1[l], w2[l], b2[l])
        return x
    x = L0_attn_x
    x = x + _layernorm(_L0_attn_ref(_layernorm(x, axis=-1), L0_attn_Wq, L0_attn_bq, L0_attn_Wk, L0_attn_bk, L0_attn_Wv), axis=-1)
    x = x + _layernorm(_L0_ffn_ref(_layernorm(x, axis=-1), L0_ffn_wqkv, L0_ffn_q_scale, L0_ffn_k_scale, L0_ffn_wo, L0_ffn_ln_g, L0_ffn_ln_b, L0_ffn_w1, L0_ffn_b1, L0_ffn_w2, L0_ffn_b2), axis=-1)
    return x

_drawn_inputs = setup_inputs


def setup_inputs(seed=0):
    import zlib

    import numpy as np

    out = dict(_drawn_inputs(seed))
    spreads = {'L0_ffn_q_scale': (1.0, 0.6),
     'L0_ffn_k_scale': (1.0, 0.6),
     'L0_ffn_ln_g': (1.0, 0.6),
     'L0_ffn_ln_b': (0.0, 0.8),
     'L0_ffn_b1': (0.0, 0.8),
     'L0_ffn_b2': (0.0, 0.8)}
    factors = {'L0_attn_bq': 7.49,
     'L0_attn_bk': 8.0,
     'L0_ffn_wqkv': 4.469,
     'L0_ffn_wo': 4.439,
     'L0_ffn_w1': 7.545,
     'L0_ffn_w2': 7.447}
    for name, (base, spread) in spreads.items():
        noise = np.random.default_rng([zlib.crc32(name.encode()), seed]).standard_normal(out[name].shape)
        drawn = base * np.exp(spread * noise) if base else spread * noise
        out[name] = jnp.asarray(drawn.astype(out[name].dtype))
    for name, factor in factors.items():
        out[name] = (out[name] * factor).astype(out[name].dtype)
    return out
```

```python
from contextlib import ExitStack
from itertools import count

import numpy as np

import concourse.bass as bass
from concourse import mybir

F32 = mybir.dt.float32
BF16 = mybir.dt.bfloat16
F32R = mybir.dt.float32r
I32 = mybir.dt.int32
ALU = mybir.AluOpType
ACT = mybir.ActivationFunctionType
AXX = mybir.AxisListType.X

P = 128
SEQS, SEQ, DIM = 16, 512, 128
TILES = SEQ // P
NT = SEQS * TILES
DEPTH, HEADS, DH, WIN = 2, 8, 64, 64
INNER = HEADS * DH
PAIRS = HEADS // 2
HID = DIM * 4 * 2 // 3
CH = 3
HC = (HID + CH) // CH
HL = HID - (CH - 1) * HC
GAMMA = 0.96875
EPS = 1e-5
MASKED = -1e30
RSQRT_SEED = float(0x5F3759DF)
NEWTON = 3
NEWTON_STEPS = 3 + 3 * NEWTON
WAITS = 16
VW = DH + 1


def shape_constants():
    p = np.arange(P)
    ident = np.eye(P, dtype=np.float32)
    shift = np.zeros((P, 2, P), np.float32)
    shift[p[:-1], 0, p[1:]] = 1.0
    shift[P - 1, 1, 0] = 1.0
    c = np.arange(SEQ)
    e = (c[None, :] - p[:, None]).astype(np.float32)
    decay = np.where(e >= 0, np.power(np.float32(GAMMA), np.maximum(e, 0)), 0).astype(np.float32)
    half = np.arange(0, DH, 2, dtype=np.float32)
    inv_freq = (np.float32(1.0) / np.power(np.float32(10000.0), half / np.float32(DH))).astype(np.float32)
    t = np.arange(SEQ, dtype=np.float32)
    freqs = np.concatenate([t[:, None] * inv_freq[None, :]] * 2, axis=-1).astype(np.float32)
    base = ((half + np.float32(0.4 * DH)) / np.float32(1.4 * DH)).astype(np.float32)
    power = ((t - SEQ // 2) / np.float32(WIN // 2)).astype(np.float32)
    scale = np.power(base[None, :], power[:, None]).astype(np.float32)
    scale = np.concatenate([scale, scale], axis=-1)
    cos, sin = np.cos(freqs), np.sin(freqs)
    sign = np.where(np.arange(DH) < DH // 2, -1.0, 1.0).astype(np.float32)
    rot = np.stack([8.0 * cos * scale, 8.0 * sin * sign * scale, cos / scale, sin * sign / scale])
    rot = rot.reshape(4, TILES, P, DH).transpose(2, 1, 0, 3)
    q = np.arange(P)[:, None] % WIN
    k = np.arange(WIN)[None, :]
    ok = np.zeros((2, P, P), bool)
    ok[:, :, :WIN] = k >= q
    ok[:, :, WIN:] = k <= q
    ok[0, :WIN, :WIN] = False
    mask = np.where(ok, 0.0, MASKED).astype(np.float32)
    mask = np.tile(mask, (1, 1, 4)).transpose(1, 0, 2)
    return {
        "ident": ident, "shift": shift.reshape(P, 2 * P), "decay": decay,
        "rot": np.ascontiguousarray(rot.reshape(P, TILES * 4 * DH), dtype=np.float32),
        "mask": np.ascontiguousarray(mask.reshape(P, 8 * P)),
    }


class Tile:

    def __init__(self, layer, batch, j):
        self.layer, self.batch, self.slot = layer, batch + j // TILES, j % TILES
        self.n = self.batch * TILES + self.slot

    def back(self, k):
        return Tile(self.layer, self.batch, self.slot - k)

    def there(self):
        return not isinstance(self.n, int) or 0 <= self.n < NT

    def done(self, per=1):
        return (self.layer * NT + self.n + 1) * per


def tile_steps(eng, layer, lag, body):
    for j in range(TILES + 1):
        body(Tile(layer, 0, j))
    with eng.Fori(1, SEQS - 1) as b:
        for j in range(1, TILES + 1):
            body(Tile(layer, b, j))
    for j in range(1, TILES + lag):
        body(Tile(layer, SEQS - 1, j))


def seq_steps(eng, lag, body):
    for s in range(lag + 1):
        body(s, s)
    with eng.Fori(lag + 1, SEQS) as s:
        body(s, None)
    for s in range(SEQS, SEQS + lag):
        body(s, s)


def on(n, back):
    return n is None or 0 <= n - back < SEQS


def past(n, back):
    return n is None or n - back >= 0


class Newton:

    def __init__(self, dve, nc, sem, base, v, half, y, tmp):
        self.dve, self.nc, self.sem, self.base = dve, nc, sem, base
        self.v, self.half, self.y, self.tmp = v, half, y, tmp

    def seed(self):
        v = self.nc.vector
        v.tensor_scalar(self.half, self.v, -0.5, None, ALU.mult).then_inc(self.sem, 1)
        v.tensor_scalar(self.tmp.bitcast(I32), self.v.bitcast(I32), 1, None, ALU.logical_shift_right).then_inc(self.sem, 1)

    def guess(self):
        self.dve.wait_ge(self.sem, self.base + 2)
        self.nc.vector.tensor_scalar(self.y.bitcast(I32), self.tmp.bitcast(I32), -1.0, RSQRT_SEED,
                                     ALU.mult, ALU.add).then_inc(self.sem, 1)

    def square(self, k):
        self.dve.wait_ge(self.sem, self.base + 3 + 3 * k)
        self.nc.vector.tensor_tensor(self.tmp, self.y, self.y, ALU.mult).then_inc(self.sem, 1)

    def times_v(self, k):
        self.dve.wait_ge(self.sem, self.base + 4 + 3 * k)
        self.nc.vector.tensor_tensor(self.tmp, self.tmp, self.half, ALU.mult).then_inc(self.sem, 1)

    def update(self, k):
        self.dve.wait_ge(self.sem, self.base + 5 + 3 * k)
        self.nc.vector.scalar_tensor_tensor(out=self.y, in0=self.tmp, scalar=1.5, in1=self.y,
                                            op0=ALU.add, op1=ALU.mult).then_inc(self.sem, 1)

    def whole(self):
        self.seed()
        self.guess()
        for k in range(NEWTON):
            self.square(k)
            self.times_v(k)
            self.update(k)


def build(nc, x, wq, wk, wv, bqk, wqkv, qks, wo, lgb, w1, b1, w2, ident, shift, decay, rot, mask, out):
    with ExitStack() as ctx:
        def sb(name, shape, dt=F32):
            return ctx.enter_context(nc.sbuf_tensor(name, shape, dt))

        def sem(name):
            return ctx.enter_context(nc.semaphore(name))

        x1 = sb("x1", [P, NT, DIM])
        xf = sb("xf", [P, NT, DIM])
        id_f = sb("id_f", [P, P])
        id_b = sb("id_b", [P, P], BF16)
        shift_s = sb("shift_s", [P, 2 * P])
        decay_s = sb("decay_s", [P, SEQ])
        rot_s = sb("rot_s", [P, TILES, 4, DH])
        mask_b = sb("mask_b", [P, 8 * P], BF16)
        wq_s, wk_s, wv_s = sb("wq_s", [P, P]), sb("wk_s", [P, P]), sb("wv_s", [P, P])
        bqk_s = sb("bqk_s", [P, 2])
        eps_s = sb("eps_s", [P, 1])
        stats = sb("stats", [P, 3, TILES, 6])
        e_stats = sb("e_stats", [P, NT, 6])
        e_tmp = sb("e_tmp", [P, 6, NT])
        mv = sb("mv", [P, 3, TILES, 2])
        std = sb("std", [P, 3, TILES])
        rstd = sb("rstd", [P, 3, TILES])
        nbias = sb("nbias", [P, 3, TILES])
        xn = sb("xn", [P, TILES, P])
        xnT = sb("xnT", [P, SEQ])
        rq, rk, rv = sb("rq", [P, SEQ]), sb("rk", [P, SEQ]), sb("rv", [P, SEQ])
        on_s = sb("on_s", [P, TILES, P])
        wqkv_s = sb("wqkv_s", [P, 3 * INNER])
        wqkv_hl = sb("wqkv_hl", [P, 2, 3 * INNER])
        wo_s = sb("wo_s", [P, INNER // P, P])
        qks_s = sb("qks_s", [P, 2, DH])
        tab = sb("tab", [P, TILES, 2, 2, DH])
        xstage = sb("xstage", [P, 2, 2, P])
        hT = sb("hT", [P, 2, SEQ + 1])
        sq = sb("sq", [P, 2 * INNER])
        ss = sb("ss", [P, 16])
        rn = sb("rn", [P, 16])
        nt_half, nt_tmp = sb("nt_half", [P, 16]), sb("nt_tmp", [P, 16])
        sT = sb("sT", [P, TILES, SEQ])
        qk_c, qk_s = sT[:, 0:2, :], sT[:, 2:4, :]
        qk_sum = sb("qk_sum", [P, 2, INNER])
        qk = sb("qk", [P, 2, INNER])
        qT = sb("qT", [P, INNER])
        kT = sb("kT", [P, PAIRS, SEQ])
        smax = sb("smax", [P, HEADS])
        prob = sb("prob", [P, HEADS, P])
        mask_f = prob[:, :, :].rearrange("p h c -> p (h c)")
        pT = sb("pT", [P, HEADS, P])
        va = sb("va", [P, TILES, HEADS, VW])
        vb = sb("vb", [P, TILES, HEADS, VW])
        rsum = sb("rsum", [P, HEADS])
        o_s = sb("o_s", [P, INNER])
        oT = sb("oT", [P, INNER])
        waited = sb("waited", [P, WAITS])
        w1_s = sb("w1_s", [P, 2 * HID])
        w2_s = sb("w2_s", [HC, CH, P])
        b1_s = sb("b1_s", [HC, 2, CH])
        lgb_s = sb("lgb_s", [P, 2])
        f_stats = sb("f_stats", [P, TILES, 2, 6])
        f_mv = sb("f_mv", [P, TILES, 2])
        f_var = sb("f_var", [P, TILES])
        f_rstd = sb("f_rstd", [P, TILES])
        f_half, f_tmp = sb("f_half", [P, TILES]), sb("f_tmp", [P, TILES])
        hn = sb("hn", [P, TILES, P])
        hnT = sb("hnT", [P, SEQ])
        gl = sb("gl", [HC, 2, SEQ])
        u = sb("u", [P, CH, SEQ])

        ps = ctx.enter_context(nc.psum_tensor("ps", [P, 8, 512], F32))

        consts_in, ret_w_in, x_in = sem("consts_in"), sem("ret_w_in"), sem("x_in")
        setup_done = sem("setup_done")
        x_st, o_st, f_st = sem("x_st"), sem("o_st"), sem("f_st")
        var_ready, std_ready, rstd_ready, scal_ready = (sem(n) for n in ("var_ready", "std_ready", "rstd_ready", "scal_ready"))
        x_scaled, xn_ready = sem("x_scaled"), sem("xn_ready")
        xnT_done, xnT_in = sem("xnT_done"), sem("xnT_in")
        proj_done, rqk_in, rv_in = sem("proj_done"), sem("rqk_in"), sem("rv_in")
        ret_s_done, decayed, ret_o_done = sem("ret_s_done"), sem("decayed"), sem("ret_o_done")
        on_ready, x1_ready = sem("on_ready"), sem("x1_ready")
        stream = sem("stream")
        attn_w_in, ffn_w_in = sem("attn_w_in"), sem("ffn_w_in")
        tab_ready = sem("tab_ready")
        wqkv_hi, wqkv_lo = sem("wqkv_hi"), sem("wqkv_lo")
        xstaged, x_lo, xT_done, hT_ready = sem("xstaged"), sem("x_lo"), sem("xT_done"), sem("hT_ready")
        qk_done, v_done, squared, v_in = sem("qk_done"), sem("v_done"), sem("squared"), sem("v_in")
        vb_in = [sem(f"vb_in{j}") for j in range(TILES)]
        rotated, summed, ss_raw, ss_ready, newt = (sem(n) for n in ("rotated", "summed", "ss_raw", "ss_ready", "newt"))
        qk_ready, qkT_done, qkT_in = sem("qk_ready"), sem("qkT_done"), sem("qkT_in")
        s_done, smax_done, p_ready = sem("s_done"), sem("smax_done"), sem("p_ready")
        pT_done, pT_in, pv_done = sem("pT_done"), sem("pT_in"), sem("pv_done")
        rsum_done, o_ready, oT_done, oT_in = sem("rsum_done"), sem("o_ready"), sem("oT_done"), sem("oT_in")
        wo_done, x_attn = sem("wo_done"), sem("x_attn")
        sh_done, f_stat, f_aggr, f_var2, f_newt = (sem(n) for n in ("sh_done", "f_stat", "f_aggr", "f_var2", "f_newt"))
        hn_ready, hnT_done, hnT_in = sem("hn_ready"), sem("hnT_done"), sem("hnT_in")
        w1_done, gelu_done, u_ready, w2_done = sem("w1_done"), sem("gelu_done"), sem("u_ready"), sem("w2_done")
        e_st, e_newt, e_nb, e_bias, e_sum, stored = (sem(n) for n in ("e_st", "e_newt", "e_nb", "e_bias", "e_sum", "stored"))

        N_CONSTS, N_RET_W, N_ATTN_W, N_FFN_W = 5, 4, 3, 4
        SETUPS = 8

        def seq_rows(t, s):
            return t[:, bass.ds(s * TILES, TILES), :]

        x_v = x.rearrange("(b t p) d -> b p t d", t=TILES, p=P)
        out_v = out.rearrange("(b t p) d -> b p t d", t=TILES, p=P)

        block = ctx.enter_context(nc.Block())

        @block.sync
        def _(sp):
            for s in range(SEQS):
                if s:
                    sp.wait_ge(x_in, 16 * s)
                nc.sync.dma_start(seq_rows(x1, s), x_v[s]).then_inc(x_in, 16)

            with sp.Fori(0, DEPTH) as l:
                def step(t):
                    if t.there():
                        sp.wait_ge(v_in, t.done())
                        nc.sync.dma_start(vb[WIN:P, t.slot], va[0:WIN, t.slot]).then_inc(vb_in[t.slot], 16)
                        if t.slot < TILES - 1:
                            nc.sync.dma_start(vb[0:WIN, t.slot + 1], va[WIN:P, t.slot]).then_inc(vb_in[t.slot + 1], 16)

                tile_steps(sp, l, 0, step)

            for s in range(SEQS):
                sp.wait_ge(e_sum, s + 1)
                nc.sync.dma_start(out_v[s], seq_rows(x1, s)).then_inc(stored, 16)
            sp.wait_ge(stored, 16 * SEQS)

        @block.gpsimd
        def _(pool):
            for i, (part, value) in enumerate((
                (hT[:, :, 0:1], 0.0),
                (va[:, :, :, DH:VW], 1.0),
                (vb[0:WIN, 0], 0.0),
                (u[96:P, CH - 1, :], 1.0),
                (eps_s[:, :], EPS),
                (mv[:, :, :, :], 1.0),
            )):
                nc.gpsimd.memset(part, value).then_inc(setup_done, 1)
                pool.wait_ge(setup_done, i + 1)

            def ret(s, n):
                if on(n, 0):
                    pool.wait_ge(scal_ready, s + 1)
                    if past(n, 1):
                        pool.wait_ge(xnT_done, s)
                    nc.gpsimd.tensor_tensor(xn[:, :, :], seq_rows(x1, s), rstd[:, 0, :].unsqueeze(2).to_broadcast([P, TILES, P]),
                                            ALU.mult).then_inc(x_scaled, 1)
                    pool.wait_ge(x_scaled, s + 1)
                    nc.gpsimd.tensor_tensor(xn[:, :, :], xn[:, :, :], nbias[:, 0, :].unsqueeze(2).to_broadcast([P, TILES, P]),
                                            ALU.add).then_inc(xn_ready, 1)
                if on(n, 3):
                    r = s - 3
                    pool.wait_ge(on_ready, r + 1)
                    nc.gpsimd.tensor_tensor(seq_rows(x1, r), seq_rows(x1, r), on_s[:, :, :], ALU.add).then_inc(x1_ready, 1)

            seq_steps(pool, 4, ret)

            with pool.Fori(0, DEPTH) as l:
                pool.wait_ge(wqkv_hi, l + 1)
                nc.gpsimd.tensor_tensor(wqkv_hl[:, 1, :].bitcast(F32R), wqkv_s[:, :], wqkv_hl[:, 0, :],
                                        ALU.subtract).then_inc(wqkv_lo, 1)

                def step(t):
                    if t.there():
                        pool.wait_ge(xstaged, t.done())
                        nc.gpsimd.tensor_tensor(xstage[:, t.slot % 2, 1, :], xf[:, t.n, :], xstage[:, t.slot % 2, 0, :],
                                                ALU.subtract).then_inc(x_lo, 1)
                    t = t.back(1)
                    if t.there():
                        pool.wait_ge(rotated, t.done())
                        if t.back(1).there():
                            pool.wait_ge(qk_ready, t.back(1).done(2))
                        nc.gpsimd.tensor_tensor(qk_sum[:, :, :], qk_c[:, :, :], qk_s[:, :, :], ALU.add).then_inc(summed, 1)
                        pool.wait_ge(summed, t.done())
                        pool.wait_ge(newt, t.done(NEWTON_STEPS))
                        if t.back(1).there():
                            pool.wait_ge(qkT_done, t.back(1).done(2))
                        for w in range(2):
                            nc.gpsimd.tensor_tensor(
                                qk[:, w, :].rearrange("p (h d) -> p h d", d=DH),
                                qk_sum[:, w, :].rearrange("p (h d) -> p h d", d=DH),
                                rn[:, w * HEADS:(w + 1) * HEADS].unsqueeze(2).to_broadcast([P, HEADS, DH]), ALU.mult).then_inc(qk_ready, 1)

                tile_steps(pool, l, 1, step)

        @block.scalar
        def _(act):
            nc.scalar.dma_start(wq_s[:, :], wq).then_inc(ret_w_in, 16)
            nc.scalar.dma_start(wk_s[:, :], wk).then_inc(ret_w_in, 16)
            nc.scalar.dma_start(wv_s[:, :], wv).then_inc(ret_w_in, 16)
            nc.scalar.dma_start(bqk_s[:, :], bqk).then_inc(ret_w_in, 16)
            nc.scalar.dma_start(id_f[:, :], ident).then_inc(consts_in, 16)
            nc.scalar.dma_start(decay_s[:, :], decay).then_inc(consts_in, 16)
            nc.scalar.dma_start(shift_s[:, :], shift).then_inc(consts_in, 16)
            nc.scalar.dma_start(rot_s[:, :, :, :], rot.rearrange("p (t a d) -> p t a d", t=TILES, a=4)).then_inc(consts_in, 16)
            nc.scalar.dma_start(mask_f, mask).then_inc(consts_in, 16)

            def load_attn(l):
                nc.scalar.dma_start(wqkv_s[:, :], wqkv[l]).then_inc(attn_w_in, 16)
                nc.scalar.dma_start(wo_s[:, :, :], wo[l].rearrange("(c p) n -> p c n", p=P)).then_inc(attn_w_in, 16)
                nc.scalar.dma_start(qks_s[:, :, :], qks[l]).then_inc(attn_w_in, 16)

            def load_ffn(l):
                nc.scalar.dma_start(w1_s[:, :], w1[l]).then_inc(ffn_w_in, 16)
                nc.scalar.dma_start(w2_s[:, :, :], w2[l]).then_inc(ffn_w_in, 16)
                nc.scalar.dma_start(b1_s[:, :, :], b1[l]).then_inc(ffn_w_in, 16)
                nc.scalar.dma_start(lgb_s[:, :], lgb[l]).then_inc(ffn_w_in, 16)

            load_attn(0)
            act.wait_ge(consts_in, 16 * N_CONSTS)
            act.wait_ge(ret_w_in, 16 * N_RET_W)
            act.wait_ge(setup_done, 6)
            nc.scalar.activation(id_b[:, :], id_f[:, :], ACT.Copy).then_inc(setup_done, 1)
            nc.scalar.activation(mask_b[:, :], mask_f, ACT.Copy).then_inc(setup_done, 1)

            def normalise(dst, src, k):
                for i in range(TILES):
                    last = nc.scalar.activation(dst(i), src(i), ACT.Identity,
                                                bias=nbias[:, k, i:i + 1], scale=rstd[:, k, i:i + 1])
                return last

            def ret(s, n):
                if on(n, 2):
                    r = s - 2
                    act.wait_ge(proj_done, 3 * r + 2)
                    if past(n, 3):
                        act.wait_ge(ret_s_done, r)
                    nc.scalar.activation(rq[:, :], ps[:, 1, :], ACT.Identity, bias=bqk_s[:, 0:1])
                    nc.scalar.activation(rk[:, :], ps[:, 2, :], ACT.Identity, bias=bqk_s[:, 1:2]).then_inc(rqk_in, 1)
                if on(n, 1):
                    r = s - 1
                    act.wait_ge(xnT_done, r + 1)
                    if past(n, 2):
                        act.wait_ge(proj_done, 3 * r)
                    nc.scalar.activation(xnT[:, :], ps[:, 0, :], ACT.Copy).then_inc(xnT_in, 1)
                if on(n, 2):
                    r = s - 2
                    act.wait_ge(proj_done, 3 * r + 3)
                    if past(n, 3):
                        act.wait_ge(ret_o_done, r)
                    nc.scalar.activation(rv[:, :], ps[:, 3, :], ACT.Copy).then_inc(rv_in, 1)
                act.wait_ge(var_ready, s + 1)
                nc.scalar.activation(std[:, :, :], mv[:, :, :, 1], ACT.Sqrt, bias=eps_s[:, 0:1]).then_inc(std_ready, 1)
                act.wait_ge(scal_ready, s + 1)
                if on(n, 3):
                    r = s - 3
                    if past(n, 4):
                        act.wait_ge(x1_ready, r)
                    normalise(lambda i: on_s[:, i, :], lambda i: ps[:, 7, i * P:(i + 1) * P], 1).then_inc(on_ready, 1)
                if on(n, 4):
                    r = s - 4
                    normalise(lambda i: xf[:, r * TILES + i, :], lambda i: x1[:, r * TILES + i, :], 2).then_inc(stream, 1)

            seq_steps(act, 4, ret)

            with act.Fori(0, DEPTH) as l:
                act.wait_ge(attn_w_in, 16 * N_ATTN_W * (l + 1))
                nc.scalar.activation(wqkv_hl[:, 0, :].bitcast(F32R), wqkv_s[:, :], ACT.Copy).then_inc(wqkv_hi, 1)
                act.wait_ge(stream, SEQS * (l + 1))
                load_ffn(l)

                def step(t):
                    if t.there():
                        if t.back(2).there():
                            act.wait_ge(xT_done, t.back(2).done())
                        nc.scalar.activation(xstage[:, t.slot % 2, 0, :].bitcast(F32R), xf[:, t.n, :], ACT.Copy).then_inc(xstaged, 1)
                    b = t.back(1)
                    if b.there():
                        act.wait_ge(qk_done, b.done())
                        if b.back(1).there():
                            act.wait_ge(ss_raw, b.back(1).done())
                        nc.scalar.activation(sq[:, :].rearrange("p (a n) -> p a n", a=2), ps[:, 0:2, :], ACT.Square).then_inc(squared, 1)
                    e = t.back(2)
                    if e.there():
                        act.wait_ge(qkT_done, 2 * e.done() - 1)
                        if e.back(1).there():
                            act.wait_ge(s_done, e.back(1).done())
                        nc.scalar.activation(qT[:, :], ps[:, 3, :], ACT.Copy)
                        act.wait_ge(qkT_done, e.done(2))
                        nc.scalar.activation(kT[:, :, e.slot * P:(e.slot + 1) * P],
                                             ps[:, 4, :].rearrange("p (i n) -> p i n", n=P), ACT.Copy).then_inc(qkT_in, 1)
                    h = t.back(3)
                    if h.there():
                        act.wait_ge(pT_done, h.done())
                        if h.back(1).there():
                            act.wait_ge(pv_done, h.back(1).done())
                        nc.scalar.activation(pT[:, :, :], ps[:, 5:7, :].rearrange("p a (h q) -> p (a h) q", q=P), ACT.Copy).then_inc(pT_in, 1)
                    m = t.back(4)
                    if m.there():
                        act.wait_ge(oT_done, m.done())
                        if m.back(1).there():
                            act.wait_ge(wo_done, m.back(1).done())
                        nc.scalar.activation(oT[:, :], ps[:, 7, :], ACT.Copy).then_inc(oT_in, 1)
                    if b.there():
                        act.wait_ge(v_done, b.done())
                        if b.back(3).there():
                            act.wait_ge(pv_done, b.back(3).done())
                        nc.scalar.activation(va[:, b.slot, :, 0:DH], ps[:, 2, :].rearrange("p (h d) -> p h d", d=DH), ACT.Copy).then_inc(v_in, 1)
                    if t.there():
                        act.wait_ge(xT_done, t.done())
                        c = t.slot * P
                        both = ps[:, 2, 0:2 * P].rearrange("p (a n) -> p a n", a=2)
                        nc.scalar.activation(hT[0:64, :, c:c + P].bitcast(F32R), both[0:64], ACT.Copy)
                        nc.scalar.activation(hT[64:P, :, c + 1:c + P + 1].bitcast(F32R), both[64:P], ACT.Copy).then_inc(hT_ready, 1)
                    if e.there():
                        act.wait_ge(smax_done, e.done())
                        if e.back(1).there():
                            act.wait_ge(pT_done, e.back(1).done())
                        for i in range(HEADS):
                            last = nc.scalar.activation(prob[:, i, :], ps[:, 3 + i // 4, i % 4 * P:(i % 4 + 1) * P], ACT.Exp,
                                                        bias=smax[:, i:i + 1])
                        last.then_inc(p_ready, 1)

                tile_steps(act, l, 4, step)

                act.wait_ge(x_attn, NT * (l + 1))
                load_attn(1 - l)
                act.wait_ge(ffn_w_in, 16 * N_FFN_W * (l + 1))

                def ffn(s, n):
                    g = l * SEQS + s
                    if on(n, 2):
                        r = g - 2
                        for c in range(CH):
                            act.wait_ge(w1_done, CH * r + c + 1)
                            rows = HC if c < CH - 1 else HL
                            if c >= 2 or past(n, 3):
                                act.wait_ge(u_ready, CH * r + c - 1)
                            nc.scalar.activation(gl[0:rows, c % 2, :], ps[0:rows, 3 + 2 * (c % 2), :], ACT.Gelu,
                                                 bias=b1_s[0:rows, 1, c:c + 1]).then_inc(gelu_done, 1)
                    if on(n, 1):
                        r = g - 1
                        act.wait_ge(hnT_done, r + 1)
                        if past(n, 2):
                            act.wait_ge(w1_done, CH * r)
                        nc.scalar.activation(hnT[:, :], ps[:, 1, :], ACT.Identity,
                                             bias=lgb_s[:, 1:2], scale=lgb_s[:, 0:1]).then_inc(hnT_in, 1)

                seq_steps(act, 2, ffn)

            act.wait_ge(attn_w_in, 16 * N_ATTN_W * (DEPTH + 1))
            act.wait_ge(e_nb, 1)
            with act.Fori(0, SEQS) as s:
                for i in range(TILES):
                    last = nc.scalar.activation(x1[:, s * TILES + i, :], x1[:, s * TILES + i, :], ACT.Identity,
                                                bias=e_tmp[:, 5, bass.ds(s * TILES + i, 1)])
                last.then_inc(e_bias, 1)

        @block.vector
        def _(dve):
            dve.wait_ge(setup_done, SETUPS)
            dve.wait_ge(consts_in, 16 * N_CONSTS)

            places = count()

            def take_wait():
                col = next(places) % WAITS
                nc.vector.memset(waited[:, col:col + 1], 0.0)

            def spread(k, src, st_sem, s):
                take_wait()
                for i in range(TILES):
                    nc.vector.bn_stats(stats[:, k, i, :], src(i)).then_inc(st_sem, 1)
                dve.wait_ge(st_sem, TILES * (s + 1))
                take_wait()
                for i in range(TILES):
                    last = nc.vector.bn_aggr(mv[:, k, i, :], stats[:, k, i, :])
                return last

            def ret(s, n):
                if on(n, 0):
                    dve.wait_ge(x_in, 16 * (s + 1))
                    last = spread(0, lambda i: x1[:, s * TILES + i, :], x_st, s)
                if on(n, 4):
                    r = s - 4
                    dve.wait_ge(x1_ready, r + 1)
                    last = spread(2, lambda i: x1[:, r * TILES + i, :], f_st, r)
                if on(n, 3):
                    r = s - 3
                    dve.wait_ge(ret_o_done, r + 1)
                    last = spread(1, lambda i: ps[:, 7, i * P:(i + 1) * P], o_st, r)
                if on(n, 0) or on(n, 4) or on(n, 3):
                    last.then_inc(var_ready, 1)
                dve.wait_ge(std_ready, s + 1)
                if past(n, 1):
                    if n is None or n <= SEQS:
                        dve.wait_ge(xn_ready, s)
                if past(n, 5):
                    dve.wait_ge(stream, s - 4)
                nc.vector.reciprocal(rstd[:, :, :], std[:, :, :]).then_inc(rstd_ready, 1)
                dve.wait_ge(rstd_ready, s + 1)
                nc.vector.scalar_tensor_tensor(out=nbias[:, :, :], in0=mv[:, :, :, 0], scalar=-1.0, in1=rstd[:, :, :],
                                               op0=ALU.mult, op1=ALU.mult).then_inc(scal_ready, 1)
                if on(n, 2):
                    r = s - 2
                    dve.wait_ge(ret_s_done, r + 1)
                    if past(n, 3):
                        dve.wait_ge(ret_o_done, r)
                    for j in range(TILES):
                        w = SEQ - j * P
                        src = ps[:, 4 + j, 0:w] if j < 3 else ps[:, 6, 2 * P:3 * P]
                        last = nc.vector.tensor_tensor(sT[:, j, 0:w], src, decay_s[:, 0:w], ALU.mult)
                    last.then_inc(decayed, 1)

            seq_steps(dve, 4, ret)

            with dve.Fori(0, DEPTH) as l:
                dve.wait_ge(stream, SEQS * (l + 1))
                dve.wait_ge(attn_w_in, 16 * N_ATTN_W * (l + 1))
                for w in range(2):
                    sc = qks_s[:, w, :].unsqueeze(1).to_broadcast([P, TILES, DH])
                    nc.vector.tensor_tensor(tab[:, :, 0, w, :], rot_s[:, :, 2 * w, :], sc, ALU.mult)
                    for a, b in ((0, 32), (32, 0)):
                        sc = qks_s[:, w, b:b + 32].unsqueeze(1).to_broadcast([P, TILES, 32])
                        last = nc.vector.tensor_tensor(tab[:, :, 1, w, a:a + 32], rot_s[:, :, 2 * w + 1, a:a + 32], sc, ALU.mult)
                last.then_inc(tab_ready, 1)
                dve.wait_ge(tab_ready, l + 1)

                def step(t):
                    k = t.back(4)
                    if k.there():
                        dve.wait_ge(pv_done, k.done())
                        ov = ps[:, 5:7, 0:4 * VW].rearrange("p a (h d) -> p a h d", d=VW)
                        nc.vector.reciprocal(rsum[:, :].rearrange("p (a h) -> p a h", a=2), ov[:, :, :, DH]).then_inc(rsum_done, 1)
                        dve.wait_ge(rsum_done, k.done())
                        if k.back(1).there():
                            dve.wait_ge(oT_done, k.back(1).done())
                        nc.vector.tensor_tensor(
                            o_s[:, :].rearrange("p (a h d) -> p a h d", a=2, d=DH), ov[:, :, :, 0:DH],
                            rsum[:, :].rearrange("p (a h) -> p a h", a=2).unsqueeze(3).to_broadcast([P, 2, 4, DH]),
                            ALU.mult).then_inc(o_ready, 1)
                    b = t.back(1)
                    e = t.back(2)
                    if b.there():
                        dve.wait_ge(squared, b.done())
                        nc.vector.tensor_reduce(out=ss[:, :], in_=sq[:, :].rearrange("p (h d) -> p h d", d=DH),
                                                axis=AXX, op=ALU.add).then_inc(ss_raw, 1)
                        if b.back(1).there():
                            dve.wait_ge(summed, b.back(1).done())
                        heads = ps[:, 0:2, :].rearrange("p a (h d) -> p a h d", d=DH)
                        oc = qk_c[:, :, :].rearrange("p a (h d) -> p a h d", d=DH)
                        os_ = qk_s[:, :, :].rearrange("p a (h d) -> p a h d", d=DH)

                        def table(k, lo, hi):
                            return tab[:, b.slot, k, :, lo:hi].unsqueeze(2).to_broadcast([P, 2, HEADS, hi - lo])

                        root = Newton(dve, nc, newt, b.back(1).done(NEWTON_STEPS), ss[:, :], nt_half[:, :], rn[:, :], nt_tmp[:, :])
                        nc.vector.tensor_tensor(oc, heads, table(0, 0, DH), ALU.mult)
                        dve.wait_ge(ss_raw, b.done())
                        nc.vector.tensor_scalar(ss[:, :], ss[:, :], 1e-24, None, ALU.max).then_inc(ss_ready, 1)
                        nc.vector.tensor_tensor(os_[:, :, :, 0:32], heads[:, :, :, 32:64], table(1, 0, 32), ALU.mult)
                        dve.wait_ge(ss_ready, b.done())
                        root.seed()
                        nc.vector.tensor_tensor(os_[:, :, :, 32:64], heads[:, :, :, 0:32], table(1, 32, 64), ALU.mult).then_inc(rotated, 1)
                        if b.back(1).there():
                            dve.wait_ge(qk_ready, b.back(1).done(2))
                        root.guess()
                        root.square(0)
                        root.times_v(0)
                        root.update(0)
                        root.square(1)
                        root.times_v(1)
                        root.update(1)
                    if e.there():
                        dve.wait_ge(s_done, e.done())
                        sc = ps[:, 3:5, :].rearrange("p a (h c) -> p a h c", c=P)
                        if e.back(1).there():
                            dve.wait_ge(p_ready, e.back(1).done())
                        nc.vector.tensor_reduce(out=smax[:, 0:4], in_=sc[:, 0], axis=AXX, op=ALU.max, negate=True)
                    if b.there():
                        root.square(2)
                    if e.there():
                        nc.vector.tensor_reduce(out=smax[:, 4:8], in_=sc[:, 1], axis=AXX, op=ALU.max, negate=True).then_inc(smax_done, 1)
                    if b.there():
                        root.times_v(2)
                        root.update(2)
                    o = t.back(4)
                    if o.there():
                        dve.wait_ge(wo_done, o.done())
                        nc.vector.tensor_tensor(xf[:, o.n, :], xf[:, o.n, :], ps[:, 7, 0:P], ALU.add).then_inc(x_attn, 1)

                tile_steps(dve, l, 4, step)

                dve.wait_ge(x_attn, NT * (l + 1))
                dve.wait_ge(ffn_w_in, 16 * N_FFN_W * (l + 1))

                def ffn(s, n):
                    g = l * SEQS + s
                    if on(n, 2):
                        r = g - 2
                        for c in range(CH):
                            dve.wait_ge(gelu_done, CH * r + c + 1)
                            if past(n, 3):
                                dve.wait_ge(w2_done, r)
                            rows = HC if c < CH - 1 else HL
                            nc.vector.scalar_tensor_tensor(
                                out=u[0:rows, c, :], in0=ps[0:rows, 2 + 2 * (c % 2), :], scalar=b1_s[0:rows, 0, c:c + 1],
                                in1=gl[0:rows, c % 2, :], op0=ALU.add, op1=ALU.mult).then_inc(u_ready, 1)
                    if on(n, 0):
                        dve.wait_ge(sh_done, g + 1)
                        take_wait()
                        for i in range(TILES):
                            nc.vector.bn_stats(f_stats[:, i, 0, :], xf[:, s * TILES + i, 0:64])
                            last = nc.vector.bn_stats(f_stats[:, i, 1, :], ps[:, 0, i * 64:(i + 1) * 64])
                        last.then_inc(f_stat, 1)
                        dve.wait_ge(f_stat, g + 1)
                        take_wait()
                        for i in range(TILES):
                            last = nc.vector.bn_aggr(f_mv[:, i, :], f_stats[:, i, :, :].rearrange("p a b -> p (a b)"))
                        last.then_inc(f_aggr, 1)
                        dve.wait_ge(f_aggr, g + 1)
                        nc.vector.tensor_scalar(f_var[:, :], f_mv[:, :, 1], EPS, None, ALU.add).then_inc(f_var2, 1)
                        dve.wait_ge(f_var2, g + 1)
                        Newton(dve, nc, f_newt, NEWTON_STEPS * g, f_var[:, :], f_half[:, :], f_rstd[:, :], f_tmp[:, :]).whole()
                        dve.wait_ge(f_newt, NEWTON_STEPS * (g + 1))
                        if past(n, 1):
                            dve.wait_ge(hnT_done, g)
                        for i in range(TILES):
                            nc.vector.tensor_scalar(hn[:, i, 0:64], xf[:, s * TILES + i, 0:64], f_mv[:, i, 0:1],
                                                    f_rstd[:, i:i + 1], ALU.subtract, ALU.mult)
                            last = nc.vector.tensor_scalar(hn[:, i, 64:P], ps[:, 0, i * 64:(i + 1) * 64], f_mv[:, i, 0:1],
                                                           f_rstd[:, i:i + 1], ALU.subtract, ALU.mult)
                        last.then_inc(hn_ready, 1)
                    if on(n, 2):
                        r = g - 2
                        dve.wait_ge(w2_done, r + 1)
                        nc.vector.tensor_tensor(seq_rows(xf, s - 2), seq_rows(xf, s - 2),
                                                ps[:, 6, :].rearrange("p (t d) -> p t d", t=TILES), ALU.add).then_inc(stream, 1)

                seq_steps(dve, 2, ffn)

            dve.wait_ge(stream, SEQS * (DEPTH + 1))
            with dve.Fori(0, SEQS) as s:
                for i in range(TILES):
                    last = nc.vector.bn_stats(e_stats[:, s * TILES + i, :], xf[:, s * TILES + i, :])
                last.then_inc(e_st, 1)
            dve.wait_ge(e_st, SEQS)
            m_even, m_odd = e_stats[:, :, 1], e_stats[:, :, 4]
            total, diff, var, half, y, nb = (e_tmp[:, i, :] for i in range(6))
            nc.vector.tensor_tensor(total, m_even, m_odd, ALU.add)
            nc.vector.tensor_tensor(var, e_stats[:, :, 2], e_stats[:, :, 5], ALU.add)
            nc.vector.tensor_tensor(diff, m_even, m_odd, ALU.subtract).then_inc(e_st, 1)
            dve.wait_ge(e_st, SEQS + 1)
            nc.vector.tensor_tensor(diff, diff, diff, ALU.mult)
            nc.vector.tensor_scalar(var, var, 1.0 / DIM, EPS, ALU.mult, ALU.add).then_inc(e_st, 1)
            dve.wait_ge(e_st, SEQS + 2)
            nc.vector.scalar_tensor_tensor(out=var, in0=diff, scalar=0.25, in1=var, op0=ALU.mult, op1=ALU.add).then_inc(e_st, 1)
            dve.wait_ge(e_st, SEQS + 3)
            Newton(dve, nc, e_newt, 0, var, half, y, diff).whole()
            dve.wait_ge(e_newt, NEWTON_STEPS)
            nc.vector.scalar_tensor_tensor(out=nb, in0=total, scalar=-0.5, in1=y, op0=ALU.mult, op1=ALU.mult).then_inc(e_nb, 1)
            with dve.Fori(0, SEQS) as s:
                dve.wait_ge(e_bias, s + 1)
                for i in range(TILES):
                    t = s * TILES + i
                    last = nc.vector.scalar_tensor_tensor(out=x1[:, t, :], in0=xf[:, t, :], scalar=e_tmp[:, 4, bass.ds(t, 1)],
                                                          in1=x1[:, t, :], op0=ALU.mult, op1=ALU.add)
                last.then_inc(e_sum, 1)

        @block.tensor
        def _(pe):
            pe.wait_ge(setup_done, SETUPS)
            pe.wait_ge(consts_in, 16 * N_CONSTS)
            pe.wait_ge(ret_w_in, 16 * N_RET_W)
            mm = nc.tensor.matmul

            def ret(s, n):
                if on(n, 2):
                    r = s - 2
                    pe.wait_ge(xnT_in, r + 1)
                    if past(n, 3):
                        pe.wait_ge(rqk_in, r)
                        pe.wait_ge(rv_in, r)
                    mm(ps[:, 1, :], wq_s[:, :], xnT[:, :], start=True, stop=True).then_inc(proj_done, 1)
                    mm(ps[:, 2, :], wk_s[:, :], xnT[:, :], start=True, stop=True).then_inc(proj_done, 1)
                    for i in range(TILES):
                        last = mm(ps[:, 3, i * P:(i + 1) * P], xnT[:, i * P:(i + 1) * P], wv_s[:, :], start=True, stop=True)
                    last.then_inc(proj_done, 1)
                if on(n, 3):
                    r = s - 3
                    pe.wait_ge(decayed, r + 1)
                    pe.wait_ge(rv_in, r + 1)
                    if past(n, 4):
                        pe.wait_ge(on_ready, r)
                    for i in range(TILES):
                        for j in range(i + 1):
                            last = mm(ps[:, 7, i * P:(i + 1) * P], sT[:, j, (i - j) * P:(i - j + 1) * P],
                                      rv[:, j * P:(j + 1) * P], start=(j == 0), stop=(j == i))
                    last.then_inc(ret_o_done, 1)
                if on(n, 1):
                    r = s - 1
                    pe.wait_ge(xn_ready, r + 1)
                    if past(n, 2):
                        pe.wait_ge(xnT_in, r)
                    for i in range(TILES):
                        last = nc.tensor.transpose(ps[:, 0, i * P:(i + 1) * P], xn[:, i, :], id_f[:, :])
                    last.then_inc(xnT_done, 1)
                if on(n, 2):
                    r = s - 2
                    pe.wait_ge(rqk_in, r + 1)
                    if past(n, 3):
                        pe.wait_ge(decayed, r)
                    for j in range(TILES):
                        w = SEQ - j * P
                        dst = ps[:, 4 + j, 0:w] if j < 3 else ps[:, 6, 2 * P:3 * P]
                        last = mm(dst, rk[:, j * P:(j + 1) * P], rq[:, j * P:SEQ], start=True, stop=True)
                    last.then_inc(ret_s_done, 1)

            seq_steps(pe, 4, ret)

            with pe.Fori(0, DEPTH) as l:
                pe.wait_ge(stream, SEQS * (l + 1))
                pe.wait_ge(attn_w_in, 16 * N_ATTN_W * (l + 1))
                pe.wait_ge(wqkv_lo, l + 1)

                def step(t):
                    d, b, h, o = t.back(2), t.back(1), t.back(3), t.back(4)
                    if b.there():
                        pe.wait_ge(hT_ready, b.done())
                        if b.back(1).there():
                            pe.wait_ge(rotated, b.back(1).done())
                            pe.wait_ge(squared, b.back(1).done())
                        c = b.slot * P
                        for banks, done in (((0, 1), qk_done), ((2,), v_done)):
                            for x_part, w_part in ((0, 0), (0, 1), (1, 0)):
                                for w in banks:
                                    last = mm(ps[:, w, :], hT[:, x_part, c:c + P].bitcast(F32R),
                                              wqkv_hl[:, w_part, w * INNER:(w + 1) * INNER].bitcast(F32R),
                                              start=(x_part + w_part == 0), stop=(x_part == 1))
                            last.then_inc(done, 1)
                    if d.there():
                        pe.wait_ge(qk_ready, 2 * d.done() - 1)
                        if d.back(1).there():
                            pe.wait_ge(p_ready, d.back(1).done())
                        for i in range(PAIRS):
                            last = nc.tensor.transpose(ps[:, 3, i * P:(i + 1) * P], qk[:, 0, i * P:(i + 1) * P], id_f[:, :])
                        last.then_inc(qkT_done, 1)
                    if o.there():
                        pe.wait_ge(o_ready, o.done())
                        if o.back(1).there():
                            pe.wait_ge(x_attn, o.back(1).done())
                        for i in range(PAIRS):
                            last = nc.tensor.transpose(ps[:, 7, i * P:(i + 1) * P], o_s[:, i * P:(i + 1) * P], id_f[:, :])
                        last.then_inc(oT_done, 1)
                    if d.there():
                        pe.wait_ge(qk_ready, d.done(2))
                        for i in range(PAIRS):
                            last = nc.tensor.transpose(ps[:, 4, i * P:(i + 1) * P], qk[:, 1, i * P:(i + 1) * P], id_f[:, :])
                        last.then_inc(qkT_done, 1)
                    if h.there():
                        pe.wait_ge(p_ready, h.done())
                        if h.back(1).there():
                            pe.wait_ge(o_ready, h.back(1).done())
                        for i in range(HEADS):
                            last = nc.tensor.transpose(ps[:, 5 + i // 4, i % 4 * P:(i % 4 + 1) * P], prob[:, i, :], id_f[:, :])
                        last.then_inc(pT_done, 1)
                    if d.there():
                        pe.wait_ge(qkT_in, d.done())
                        for par in range(2):
                            mm(ps[:, 3 + par, :], id_b[:, :], mask_b[:, (1 if d.slot else 0) * 512:(1 if d.slot else 0) * 512 + 512],
                               start=True, stop=False, skip_group_check=True)
                        for i in range(PAIRS):
                            for half in range(2):
                                first = d.slot == 0 and half == 0
                                lo = d.slot * P + (0 if first else (half - 1) * WIN)
                                hi = d.slot * P + (half + 1) * WIN
                                for par in range(2):
                                    r = slice(par * DH, (par + 1) * DH)
                                    last = mm(ps[half * WIN:(half + 1) * WIN, 3 + par, (i + 1) * P - (hi - lo):(i + 1) * P],
                                              qT[r, i * P + half * WIN:i * P + (half + 1) * WIN], kT[r, i, lo:hi],
                                              start=False, stop=(i == PAIRS - 1), skip_group_check=True)
                        last.then_inc(s_done, 1)
                    if o.there():
                        pe.wait_ge(oT_in, o.done())
                        for i in range(PAIRS):
                            last = mm(ps[:, 7, 0:P], oT[:, i * P:(i + 1) * P], wo_s[:, i, :], start=(i == 0), stop=(i == PAIRS - 1))
                        last.then_inc(wo_done, 1)

                    if t.there():
                        pe.wait_ge(x_lo, t.done())
                        if t.back(1).there():
                            pe.wait_ge(v_in, t.back(1).done())
                        nc.tensor.transpose(ps[:, 2, 0:P], xstage[:, t.slot % 2, 0, :], id_f[:, :])
                        nc.tensor.transpose(ps[:, 2, P:2 * P], xstage[:, t.slot % 2, 1, :], id_f[:, :]).then_inc(xT_done, 1)
                    if h.there():
                        pe.wait_ge(pT_in, h.done())
                        pe.wait_ge(vb_in[h.slot], (16 if h.slot == 0 else 32) * (h.layer * SEQS + h.batch + 1))
                        for i in range(HEADS):
                            j = i % 2 * PAIRS + i // 2
                            col = i % 4 * VW
                            mm(ps[0:WIN, 5 + i // 4, col:col + VW], pT[:, j, 0:WIN], vb[:, h.slot, i, :], start=True, stop=True)
                            last = mm(ps[WIN:P, 5 + i // 4, col:col + VW], pT[:, j, WIN:P], va[:, h.slot, i, :], start=True, stop=True)
                        last.then_inc(pv_done, 1)

                tile_steps(pe, l, 4, step)

                pe.wait_ge(x_attn, NT * (l + 1))
                pe.wait_ge(ffn_w_in, 16 * N_FFN_W * (l + 1))

                def ffn(s, n):
                    g = l * SEQS + s
                    if on(n, 2):
                        r = g - 2
                        for c in range(CH):
                            rows = HC if c < CH - 1 else HL
                            if c == 0:
                                pe.wait_ge(hnT_in, r + 1)
                            if c >= 2 or past(n, 3):
                                pe.wait_ge(u_ready, CH * r + c - 1)
                            mm(ps[0:rows, 2 + 2 * (c % 2), :], w1_s[:, c * HC:c * HC + rows], hnT[:, :], start=True, stop=True)
                            mm(ps[0:rows, 3 + 2 * (c % 2), :], w1_s[:, HID + c * HC:HID + c * HC + rows], hnT[:, :],
                               start=True, stop=True).then_inc(w1_done, 1)
                    if on(n, 0):
                        if past(n, 1):
                            pe.wait_ge(hn_ready, g)
                        for i in range(TILES):
                            mm(ps[:, 0, i * 64:(i + 1) * 64], shift_s[:, 0:P], xf[:, s * TILES + i, 64:P], start=True, stop=(i == 0))
                            if i:
                                last = mm(ps[:, 0, i * 64:(i + 1) * 64], shift_s[:, P:2 * P], xf[:, s * TILES + i - 1, 64:P], start=False, stop=True)
                        last.then_inc(sh_done, 1)
                    if on(n, 1):
                        r = g - 1
                        pe.wait_ge(hn_ready, r + 1)
                        if past(n, 2):
                            pe.wait_ge(hnT_in, r)
                        for i in range(TILES):
                            last = nc.tensor.transpose(ps[:, 1, i * P:(i + 1) * P], hn[:, i, :], id_f[:, :])
                        last.then_inc(hnT_done, 1)
                    if on(n, 2):
                        r = g - 2
                        pe.wait_ge(u_ready, CH * (r + 1))
                        if past(n, 3):
                            pe.wait_ge(stream, SEQS + r)
                        for i in range(TILES):
                            for c in range(CH):
                                last = mm(ps[:, 6, i * P:(i + 1) * P], u[0:HC, c, i * P:(i + 1) * P], w2_s[:, c, :],
                                          start=(c == 0), stop=(c == CH - 1))
                        last.then_inc(w2_done, 1)

                seq_steps(pe, 2, ffn)


def kernel(L0_attn_x, L0_attn_Wq, L0_attn_bq, L0_attn_Wk, L0_attn_bk, L0_attn_Wv, L0_ffn_wqkv, L0_ffn_q_scale,
           L0_ffn_k_scale, L0_ffn_wo, L0_ffn_ln_g, L0_ffn_ln_b, L0_ffn_w1, L0_ffn_b1, L0_ffn_w2, L0_ffn_b2):
    import concourse.bacc as bacc
    from concourse.bass_utils import run_bass_kernel_spmd

    a = np.asarray
    b1 = np.zeros((DEPTH, 2, CH * HC), np.float32)
    b1[:, :, 0:HID] = a(L0_ffn_b1).reshape(DEPTH, 2, HID)
    w2 = np.concatenate([a(L0_ffn_w2), a(L0_ffn_b2)[:, None, :]], axis=1)
    qks = np.stack([a(L0_ffn_q_scale), a(L0_ffn_k_scale)], axis=1)
    arrays = {
        "x": a(L0_attn_x).reshape(SEQS * SEQ, DIM),
        "wq": a(L0_attn_Wq).T, "wk": a(L0_attn_Wk).T, "wv": a(L0_attn_Wv).T,
        "bqk": np.stack([a(L0_attn_bq), a(L0_attn_bk)], axis=1),
        "wqkv": a(L0_ffn_wqkv),
        "qks": np.broadcast_to(qks[:, None], (DEPTH, P, 2, DH)),
        "wo": a(L0_ffn_wo),
        "lgb": np.stack([a(L0_ffn_ln_g), a(L0_ffn_ln_b)], axis=2),
        "w1": a(L0_ffn_w1),
        "b1": b1.reshape(DEPTH, 2, CH, HC).transpose(0, 3, 1, 2),
        "w2": w2.reshape(DEPTH, CH, HC, P).transpose(0, 2, 1, 3),
        **shape_constants(),
    }
    nc = bacc.Bacc("TRN2", target_bir_lowering=False, num_devices=1)
    args, sent = [], {}
    for name, v in arrays.items():
        v = np.ascontiguousarray(v)
        sent[f"in_{name}_dram"] = v
        args.append(nc.dram_tensor(f"in_{name}_dram", v.shape, mybir.dt.from_np(v.dtype), kind="ExternalInput").ap())
    args.append(nc.dram_tensor("out_0_dram", (SEQS * SEQ, DIM), F32, kind="ExternalOutput").ap())
    build(nc, *args)
    r = run_bass_kernel_spmd(nc, [sent], core_ids=[0])
    return r.results[0]["out_0_dram"].reshape(SEQS, SEQ, DIM)
```

```python
from contextlib import ExitStack
from itertools import count

import numpy as np

import concourse.bass as bass
from concourse import mybir

F32 = mybir.dt.float32
BF16 = mybir.dt.bfloat16
F32R = mybir.dt.float32r
I32 = mybir.dt.int32
ALU = mybir.AluOpType
ACT = mybir.ActivationFunctionType
AXX = mybir.AxisListType.X

P = 128
SEQS, SEQ, DIM = 16, 512, 128
TILES = SEQ // P
NT = SEQS * TILES
DEPTH, HEADS, DH, WIN = 2, 8, 64, 64
INNER = HEADS * DH
PAIRS = HEADS // 2
HID = DIM * 4 * 2 // 3
CH = 3
HC = (HID + CH) // CH
HL = HID - (CH - 1) * HC
GAMMA = 0.96875
EPS = 1e-5
MASKED = -1e30
RSQRT_SEED = float(0x5F3759DF)
NEWTON = 3
NEWTON_STEPS = 3 + 3 * NEWTON
WAITS = 16


def shape_constants():
    p = np.arange(P)
    ident = np.eye(P, dtype=np.float32)
    shift = np.zeros((P, 5, P), np.float32)
    shift[p[:-1], 0, p[1:]] = 1.0
    shift[P - 1, 1, 0] = 1.0
    shift[p[1:], 2, p[:-1]] = 1.0
    shift[0, 3, P - 1] = 1.0
    shift[0, 4, :] = 1.0
    c = np.arange(SEQ)
    e = (c[None, :] - p[:, None]).astype(np.float32)
    decay = np.where(e >= 0, np.power(np.float32(GAMMA), np.maximum(e, 0)), 0).astype(np.float32)
    half = np.arange(0, DH, 2, dtype=np.float32)
    inv_freq = (np.float32(1.0) / np.power(np.float32(10000.0), half / np.float32(DH))).astype(np.float32)
    t = np.arange(SEQ, dtype=np.float32)
    freqs = np.concatenate([t[:, None] * inv_freq[None, :]] * 2, axis=-1).astype(np.float32)
    base = ((half + np.float32(0.4 * DH)) / np.float32(1.4 * DH)).astype(np.float32)
    power = ((t - SEQ // 2) / np.float32(WIN // 2)).astype(np.float32)
    scale = np.power(base[None, :], power[:, None]).astype(np.float32)
    scale = np.concatenate([scale, scale], axis=-1)
    cos, sin = np.cos(freqs), np.sin(freqs)
    sign = np.where(np.arange(DH) < DH // 2, -1.0, 1.0).astype(np.float32)
    rot = np.stack([8.0 * cos * scale, 8.0 * sin * sign * scale, cos / scale, sin * sign / scale])
    rot = rot.reshape(4, TILES, P, DH).transpose(2, 1, 0, 3)
    q = np.arange(P)[:, None] % WIN
    k = np.arange(WIN)[None, :]
    ok = np.zeros((2, P, P), bool)
    ok[:, :, :WIN] = k >= q
    ok[:, :, WIN:] = k <= q
    ok[0, :WIN, :WIN] = False
    mask = np.where(ok, 0.0, MASKED).astype(np.float32)
    mask = np.tile(mask, (1, 1, 4)).transpose(1, 0, 2)
    return {
        "ident": ident, "shift": shift.reshape(P, 5 * P), "decay": decay,
        "rot": np.ascontiguousarray(rot.reshape(P, TILES * 4 * DH), dtype=np.float32),
        "mask": np.ascontiguousarray(mask.reshape(P, 8 * P)),
    }


class Tile:

    def __init__(self, layer, batch, j):
        self.layer, self.batch, self.slot = layer, batch + j // TILES, j % TILES
        self.n = self.batch * TILES + self.slot

    def back(self, k):
        return Tile(self.layer, self.batch, self.slot - k)

    def there(self):
        return not isinstance(self.n, int) or 0 <= self.n < NT

    def done(self, per=1):
        return (self.layer * NT + self.n + 1) * per


def tile_steps(eng, layer, lag, body):
    for j in range(TILES + 1):
        body(Tile(layer, 0, j))
    with eng.Fori(1, SEQS - 1) as b:
        for j in range(1, TILES + 1):
            body(Tile(layer, b, j))
    for j in range(1, TILES + lag):
        body(Tile(layer, SEQS - 1, j))


def seq_steps(eng, lag, body):
    for s in range(lag + 1):
        body(s, s)
    with eng.Fori(lag + 1, SEQS) as s:
        body(s, None)
    for s in range(SEQS, SEQS + lag):
        body(s, s)


def on(n, back):
    return n is None or 0 <= n - back < SEQS


def past(n, back):
    return n is None or n - back >= 0


class Newton:

    def __init__(self, dve, nc, sem, base, v, half, y, tmp):
        self.dve, self.nc, self.sem, self.base = dve, nc, sem, base
        self.v, self.half, self.y, self.tmp = v, half, y, tmp

    def seed(self):
        v = self.nc.vector
        v.tensor_scalar(self.half, self.v, -0.5, None, ALU.mult).then_inc(self.sem, 1)
        v.tensor_scalar(self.tmp.bitcast(I32), self.v.bitcast(I32), 1, None, ALU.logical_shift_right).then_inc(self.sem, 1)

    def guess(self):
        self.dve.wait_ge(self.sem, self.base + 2)
        self.nc.vector.tensor_scalar(self.y.bitcast(I32), self.tmp.bitcast(I32), -1.0, RSQRT_SEED,
                                     ALU.mult, ALU.add).then_inc(self.sem, 1)

    def square(self, k):
        self.dve.wait_ge(self.sem, self.base + 3 + 3 * k)
        self.nc.vector.tensor_tensor(self.tmp, self.y, self.y, ALU.mult).then_inc(self.sem, 1)

    def times_v(self, k):
        self.dve.wait_ge(self.sem, self.base + 4 + 3 * k)
        self.nc.vector.tensor_tensor(self.tmp, self.tmp, self.half, ALU.mult).then_inc(self.sem, 1)

    def update(self, k):
        self.dve.wait_ge(self.sem, self.base + 5 + 3 * k)
        self.nc.vector.scalar_tensor_tensor(out=self.y, in0=self.tmp, scalar=1.5, in1=self.y,
                                            op0=ALU.add, op1=ALU.mult).then_inc(self.sem, 1)

    def whole(self):
        self.seed()
        self.guess()
        for k in range(NEWTON):
            self.square(k)
            self.times_v(k)
            self.update(k)


def build(nc, x, wq, wk, wv, bqk, wqkv, qks, wo, lgb, w1, b1, w2, ident, shift, decay, rot, mask, out):
    with ExitStack() as ctx:
        def sb(name, shape, dt=F32):
            return ctx.enter_context(nc.sbuf_tensor(name, shape, dt))

        def sem(name):
            return ctx.enter_context(nc.semaphore(name))

        x1 = sb("x1", [P, NT, DIM])
        xf = sb("xf", [P, NT, DIM])
        id_f = sb("id_f", [P, P])
        id_b = sb("id_b", [P, P], BF16)
        shift_s = sb("shift_s", [P, 5, P])
        decay_s = sb("decay_s", [P, SEQ])
        rot_s = sb("rot_s", [P, TILES, 4, DH])
        mask_b = sb("mask_b", [P, 8 * P], BF16)
        wq_s, wk_s, wv_s = sb("wq_s", [P, P]), sb("wk_s", [P, P]), sb("wv_s", [P, P])
        bqk_s = sb("bqk_s", [P, 2])
        eps_s = sb("eps_s", [P, 1])
        stats = sb("stats", [P, 3, TILES, 6])
        e_tmp = sb("e_tmp", [P, 6, NT])
        mv = sb("mv", [P, 3, TILES, 2])
        std = sb("std", [P, 3, TILES])
        rstd = sb("rstd", [P, 3, TILES])
        nbias = sb("nbias", [P, 3, TILES])
        xn = sb("xn", [P, TILES, P])
        xnT = sb("xnT", [P, SEQ])
        rq, rk, rv = sb("rq", [P, SEQ]), sb("rk", [P, SEQ]), sb("rv", [P, SEQ])
        on_s = sb("on_s", [P, TILES, P])
        wqkv_s = sb("wqkv_s", [P, 3 * INNER])
        wqkv_hl = sb("wqkv_hl", [P, 2, 3 * INNER])
        wo_s = sb("wo_s", [P, INNER // P, P])
        qks_s = sb("qks_s", [P, 2, DH])
        tab = sb("tab", [P, TILES, 2, 2, DH])
        xstage = sb("xstage", [P, 2, 2, P])
        hT = sb("hT", [P, 2, SEQ + 1])
        sq = sb("sq", [P, 2 * INNER])
        ss = sb("ss", [P, 16])
        rn = sb("rn", [P, 16])
        nt_half, nt_tmp = sb("nt_half", [P, 16]), sb("nt_tmp", [P, 16])
        sT = sb("sT", [P, TILES, SEQ])
        qk_c, qk_s = sT[:, 0:2, :], sT[:, 2:4, :]
        qk_sum = sb("qk_sum", [P, 2, INNER])
        qk = sb("qk", [P, 2, INNER])
        qT = sb("qT", [P, INNER])
        kT = sb("kT", [P, PAIRS, SEQ])
        smax = sb("smax", [P, HEADS])
        prob = sb("prob", [P, HEADS, P])
        mask_f = prob[:, :, :].rearrange("p h c -> p (h c)")
        pT = sb("pT", [P, HEADS, P])
        va = sb("va", [P, TILES, HEADS, DH])
        vb = sb("vb", [P, TILES, HEADS, DH])
        psum_p, rsum = sb("psum_p", [P, HEADS]), sb("rsum", [P, HEADS])
        oT = sb("oT", [P, INNER])
        waited = sb("waited", [P, WAITS])
        w1_s = sb("w1_s", [P, 2 * HID])
        w1_hl = sb("w1_hl", [P, 2, 2 * HID])
        w2_s = sb("w2_s", [HC, CH, P])
        b1_s = sb("b1_s", [HC, 2, CH])
        lgb_s = sb("lgb_s", [P, 2])
        h_stats = sb("h_stats", [P, 2, NT, 6])
        e_stats = h_stats[:, 0]
        h_mom = sb("h_mom", [P, 2, 2, NT])
        h_diff = sb("h_diff", [P, 2, NT])
        norm = sb("norm", [P, 2, NT, 2])
        norm0 = sb("norm0", [P, SEQS])
        hn = xn
        hnT = sb("hnT", [P, SEQ + 1])
        hnT_hl = sb("hnT_hl", [P, 2, SEQ])
        gl = qk[0:HC]
        u = sb("u", [P, CH, SEQ])

        ps = ctx.enter_context(nc.psum_tensor("ps", [P, 8, 512], F32))

        consts_in, ret_w_in, x_in = sem("consts_in"), sem("ret_w_in"), sem("x_in")
        setup_done = sem("setup_done")
        x_st, o_st, f_st = sem("x_st"), sem("o_st"), sem("f_st")
        var_ready, std_ready, rstd_ready, scal_ready = (sem(n) for n in ("var_ready", "std_ready", "rstd_ready", "scal_ready"))
        x_scaled, xn_ready = sem("x_scaled"), sem("xn_ready")
        xnT_done, xnT_in = sem("xnT_done"), sem("xnT_in")
        proj_done, rqk_in, rv_in = sem("proj_done"), sem("rqk_in"), sem("rv_in")
        ret_s_done, decayed, ret_o_done = sem("ret_s_done"), sem("decayed"), sem("ret_o_done")
        on_ready, x1_ready = sem("on_ready"), sem("x1_ready")
        stream = sem("stream")
        attn_w_in, ffn_w_in = sem("attn_w_in"), sem("ffn_w_in")
        tab_ready = sem("tab_ready")
        wqkv_hi, wqkv_lo = sem("wqkv_hi"), sem("wqkv_lo")
        xstaged, x_lo, xT_done, hT_ready = sem("xstaged"), sem("x_lo"), sem("xT_done"), sem("hT_ready")
        qk_done, v_done, squared, v_in = sem("qk_done"), sem("v_done"), sem("squared"), sem("v_in")
        vb_in = [sem(f"vb_in{j}") for j in range(TILES)]
        rotated, summed, ss_raw, ss_ready, newt = (sem(n) for n in ("rotated", "summed", "ss_raw", "ss_ready", "newt"))
        qk_ready, qkT_done, qkT_in = sem("qk_ready"), sem("qkT_done"), sem("qkT_in")
        s_done, smax_done, p_ready = sem("s_done"), sem("smax_done"), sem("p_ready")
        pT_done, pT_in, pv_done = sem("pT_done"), sem("pT_in"), sem("pv_done")
        rsum_ready, pn_ready, oT_in = sem("rsum_ready"), sem("pn_ready"), sem("oT_in")
        wo_done, x_attn = sem("wo_done"), sem("x_attn")
        h_st, h_step, mom_ready, mom_moved = sem("h_st"), sem("h_step"), sem("mom_ready"), sem("mom_moved")
        f_newt, norm_own, norm_moved, norm_ready = sem("f_newt"), sem("norm_own"), sem("norm_moved"), sem("norm_ready")
        w1_hi, w1_lo, hn_scaled = sem("w1_hi"), sem("w1_lo"), sem("hn_scaled")
        hn_ready, hnT_done, hnT_in = sem("hn_ready"), sem("hnT_done"), sem("hnT_in")
        hnT_hi, hnT_lo = sem("hnT_hi"), sem("hnT_lo")
        w1_done, gelu_done, u_ready, w2_done = sem("w1_done"), sem("gelu_done"), sem("u_ready"), sem("w2_done")
        e_st, e_newt, e_nb, e_bias, e_sum, stored = (sem(n) for n in ("e_st", "e_newt", "e_nb", "e_bias", "e_sum", "stored"))

        N_CONSTS, N_RET_W, N_ATTN_W, N_FFN_W = 5, 4, 3, 4
        SETUPS = 7
        H_STEPS = 5

        def seq_rows(t, s):
            return t[:, bass.ds(s * TILES, TILES), :]

        x_v = x.rearrange("(b t p) d -> b p t d", t=TILES, p=P)
        out_v = out.rearrange("(b t p) d -> b p t d", t=TILES, p=P)

        block = ctx.enter_context(nc.Block())

        @block.sync
        def _(sp):
            for s in range(SEQS):
                if s:
                    sp.wait_ge(x_in, 16 * s)
                nc.sync.dma_start(seq_rows(x1, s), x_v[s]).then_inc(x_in, 16)

            with sp.Fori(0, DEPTH) as l:
                def step(t):
                    if t.there():
                        sp.wait_ge(v_in, t.done())
                        nc.sync.dma_start(vb[WIN:P, t.slot], va[0:WIN, t.slot]).then_inc(vb_in[t.slot], 16)
                        if t.slot < TILES - 1:
                            nc.sync.dma_start(vb[0:WIN, t.slot + 1], va[WIN:P, t.slot]).then_inc(vb_in[t.slot + 1], 16)

                tile_steps(sp, l, 0, step)

            for s in range(SEQS):
                sp.wait_ge(e_sum, s + 1)
                nc.sync.dma_start(out_v[s], seq_rows(x1, s)).then_inc(stored, 16)
            sp.wait_ge(stored, 16 * SEQS)

        @block.gpsimd
        def _(pool):
            for i, (part, value) in enumerate((
                (hT[:, :, 0:1], 0.0),
                (vb[0:WIN, 0], 0.0),
                (u[96:P, CH - 1, :], 1.0),
                (eps_s[:, :], EPS),
                (mv[:, :, :, :], 1.0),
            )):
                nc.gpsimd.memset(part, value).then_inc(setup_done, 1)
                pool.wait_ge(setup_done, i + 1)

            def ret(s, n):
                if on(n, 0):
                    pool.wait_ge(scal_ready, s + 1)
                    if past(n, 1):
                        pool.wait_ge(xnT_done, s)
                    nc.gpsimd.tensor_tensor(xn[:, :, :], seq_rows(x1, s), rstd[:, 0, :].unsqueeze(2).to_broadcast([P, TILES, P]),
                                            ALU.mult).then_inc(x_scaled, 1)
                    pool.wait_ge(x_scaled, s + 1)
                    nc.gpsimd.tensor_tensor(xn[:, :, :], xn[:, :, :], nbias[:, 0, :].unsqueeze(2).to_broadcast([P, TILES, P]),
                                            ALU.add).then_inc(xn_ready, 1)
                if on(n, 3):
                    r = s - 3
                    pool.wait_ge(on_ready, r + 1)
                    nc.gpsimd.tensor_tensor(seq_rows(x1, r), seq_rows(x1, r), on_s[:, :, :], ALU.add).then_inc(x1_ready, 1)

            seq_steps(pool, 4, ret)

            with pool.Fori(0, DEPTH) as l:
                pool.wait_ge(wqkv_hi, l + 1)
                nc.gpsimd.tensor_tensor(wqkv_hl[:, 1, :].bitcast(F32R), wqkv_s[:, :], wqkv_hl[:, 0, :],
                                        ALU.subtract).then_inc(wqkv_lo, 1)

                def split(t):
                    if t.there():
                        pool.wait_ge(xstaged, t.done())
                        nc.gpsimd.tensor_tensor(xstage[:, t.slot % 2, 1, :], xf[:, t.n, :], xstage[:, t.slot % 2, 0, :],
                                                ALU.subtract).then_inc(x_lo, 1)

                def step(t):
                    following = t.back(-1)
                    h = t.back(3)
                    if h.there():
                        for a in range(2):
                            pool.wait_ge(rsum_ready, 2 * h.done() - 1 + a)
                            part = prob[:, a * PAIRS:(a + 1) * PAIRS, :]
                            nc.gpsimd.tensor_tensor(part, part, rsum[:, a * PAIRS:(a + 1) * PAIRS].unsqueeze(2).to_broadcast(
                                [P, PAIRS, P]), ALU.mult).then_inc(pn_ready, 1)
                    t = t.back(1)
                    if t.there():
                        pool.wait_ge(rotated, t.done())
                        if t.back(1).there():
                            pool.wait_ge(qk_ready, t.back(1).done(2))
                        nc.gpsimd.tensor_tensor(qk_sum[:, :, :], qk_c[:, :, :], qk_s[:, :, :], ALU.add).then_inc(summed, 1)
                        pool.wait_ge(summed, t.done())
                        pool.wait_ge(newt, t.done(NEWTON_STEPS))
                        if t.back(1).there():
                            pool.wait_ge(qkT_done, t.back(1).done(2))
                        for w in range(2):
                            nc.gpsimd.tensor_tensor(
                                qk[:, w, :].rearrange("p (h d) -> p h d", d=DH),
                                qk_sum[:, w, :].rearrange("p (h d) -> p h d", d=DH),
                                rn[:, w * HEADS:(w + 1) * HEADS].unsqueeze(2).to_broadcast([P, HEADS, DH]), ALU.mult).then_inc(qk_ready, 1)
                    split(following)

                split(Tile(l, 0, 0))
                tile_steps(pool, l, 3, step)

                pool.wait_ge(w1_hi, l + 1)
                nc.gpsimd.tensor_tensor(w1_hl[:, 1, :].bitcast(F32R), w1_s[:, :], w1_hl[:, 0, :],
                                        ALU.subtract).then_inc(w1_lo, 1)
                pool.wait_ge(norm_ready, l + 1)

                def ffn(s, n):
                    g = l * SEQS + s
                    xs = seq_rows(xf, s).rearrange("p t (a d) -> p (t a) d", a=2)
                    hs = hn[:, :, :].rearrange("p t (a d) -> p (t a) d", a=2)

                    def scalars(k):
                        return norm[:, k, bass.ds(s * TILES, TILES), :].rearrange("p t a -> p (t a)").unsqueeze(2).to_broadcast(
                            [P, 2 * TILES, DIM // 2])

                    if past(n, 1):
                        pool.wait_ge(hnT_done, g)
                    nc.gpsimd.tensor_tensor(hs, xs, scalars(0), ALU.mult).then_inc(hn_scaled, 1)
                    pool.wait_ge(hn_scaled, g + 1)
                    nc.gpsimd.tensor_tensor(hs, hs, scalars(1), ALU.add).then_inc(hn_ready, 1)

                seq_steps(pool, 0, ffn)

        @block.scalar
        def _(act):
            nc.scalar.dma_start(wq_s[:, :], wq).then_inc(ret_w_in, 16)
            nc.scalar.dma_start(wk_s[:, :], wk).then_inc(ret_w_in, 16)
            nc.scalar.dma_start(wv_s[:, :], wv).then_inc(ret_w_in, 16)
            nc.scalar.dma_start(bqk_s[:, :], bqk).then_inc(ret_w_in, 16)
            nc.scalar.dma_start(id_f[:, :], ident).then_inc(consts_in, 16)
            nc.scalar.dma_start(decay_s[:, :], decay).then_inc(consts_in, 16)
            nc.scalar.dma_start(shift_s[:, :, :], shift.rearrange("p (a n) -> p a n", a=5)).then_inc(consts_in, 16)
            nc.scalar.dma_start(rot_s[:, :, :, :], rot.rearrange("p (t a d) -> p t a d", t=TILES, a=4)).then_inc(consts_in, 16)
            nc.scalar.dma_start(mask_f, mask).then_inc(consts_in, 16)

            def load_attn(l):
                nc.scalar.dma_start(wqkv_s[:, :], wqkv[l]).then_inc(attn_w_in, 16)
                nc.scalar.dma_start(wo_s[:, :, :], wo[l].rearrange("(c p) n -> p c n", p=P)).then_inc(attn_w_in, 16)
                nc.scalar.dma_start(qks_s[:, :, :], qks[l]).then_inc(attn_w_in, 16)

            def load_ffn(l):
                nc.scalar.dma_start(w1_s[:, :], w1[l]).then_inc(ffn_w_in, 16)
                nc.scalar.dma_start(w2_s[:, :, :], w2[l]).then_inc(ffn_w_in, 16)
                nc.scalar.dma_start(b1_s[:, :, :], b1[l]).then_inc(ffn_w_in, 16)
                nc.scalar.dma_start(lgb_s[:, :], lgb[l]).then_inc(ffn_w_in, 16)

            load_attn(0)
            act.wait_ge(consts_in, 16 * N_CONSTS)
            act.wait_ge(ret_w_in, 16 * N_RET_W)
            act.wait_ge(setup_done, SETUPS - 2)
            nc.scalar.activation(id_b[:, :], id_f[:, :], ACT.Copy).then_inc(setup_done, 1)
            nc.scalar.activation(mask_b[:, :], mask_f, ACT.Copy).then_inc(setup_done, 1)

            def normalise(dst, src, k):
                for i in range(TILES):
                    last = nc.scalar.activation(dst(i), src(i), ACT.Identity,
                                                bias=nbias[:, k, i:i + 1], scale=rstd[:, k, i:i + 1])
                return last

            def ret(s, n):
                if on(n, 2):
                    r = s - 2
                    act.wait_ge(proj_done, 3 * r + 2)
                    if past(n, 3):
                        act.wait_ge(ret_s_done, r)
                    nc.scalar.activation(rq[:, :], ps[:, 1, :], ACT.Identity, bias=bqk_s[:, 0:1])
                    nc.scalar.activation(rk[:, :], ps[:, 2, :], ACT.Identity, bias=bqk_s[:, 1:2]).then_inc(rqk_in, 1)
                if on(n, 1):
                    r = s - 1
                    act.wait_ge(xnT_done, r + 1)
                    if past(n, 2):
                        act.wait_ge(proj_done, 3 * r)
                    nc.scalar.activation(xnT[:, :], ps[:, 0, :], ACT.Copy).then_inc(xnT_in, 1)
                if on(n, 2):
                    r = s - 2
                    act.wait_ge(proj_done, 3 * r + 3)
                    if past(n, 3):
                        act.wait_ge(ret_o_done, r)
                    nc.scalar.activation(rv[:, :], ps[:, 3, :], ACT.Copy).then_inc(rv_in, 1)
                act.wait_ge(var_ready, s + 1)
                nc.scalar.activation(std[:, :, :], mv[:, :, :, 1], ACT.Sqrt, bias=eps_s[:, 0:1]).then_inc(std_ready, 1)
                act.wait_ge(scal_ready, s + 1)
                if on(n, 3):
                    r = s - 3
                    if past(n, 4):
                        act.wait_ge(x1_ready, r)
                    normalise(lambda i: on_s[:, i, :], lambda i: ps[:, 7, i * P:(i + 1) * P], 1).then_inc(on_ready, 1)
                if on(n, 4):
                    r = s - 4
                    normalise(lambda i: xf[:, r * TILES + i, :], lambda i: x1[:, r * TILES + i, :], 2).then_inc(stream, 1)

            seq_steps(act, 4, ret)

            with act.Fori(0, DEPTH) as l:
                act.wait_ge(attn_w_in, 16 * N_ATTN_W * (l + 1))
                nc.scalar.activation(wqkv_hl[:, 0, :].bitcast(F32R), wqkv_s[:, :], ACT.Copy).then_inc(wqkv_hi, 1)
                act.wait_ge(stream, SEQS * (l + 1))
                load_ffn(l)

                def exponentials(t, a):
                    act.wait_ge(smax_done, 2 * t.done() - 1 + a)
                    if t.back(1).there():
                        act.wait_ge(pT_done, 2 * t.back(1).done() - 1 + a)
                    for i in range(PAIRS):
                        j = a * PAIRS + i
                        last = nc.scalar.activation(prob[:, j, :], ps[:, 3 + a, i * P:(i + 1) * P], ACT.Exp,
                                                    bias=smax[:, j:j + 1], accum_out=psum_p[:, j:j + 1])
                    last.then_inc(p_ready, 1)

                def fetch_pT(t, a):
                    act.wait_ge(pT_done, 2 * t.done() - 1 + a)
                    if t.back(1).there():
                        act.wait_ge(pv_done, t.back(1).done())
                    nc.scalar.activation(pT[:, a * PAIRS:(a + 1) * PAIRS, :], ps[:, 5 + a, :].rearrange("p (h q) -> p h q", q=P),
                                         ACT.Copy).then_inc(pT_in, 1)

                def stage(t):
                    if t.there():
                        if t.back(2).there():
                            act.wait_ge(xT_done, t.back(2).done())
                        nc.scalar.activation(xstage[:, t.slot % 2, 0, :].bitcast(F32R), xf[:, t.n, :], ACT.Copy).then_inc(xstaged, 1)

                def step(t):
                    b, e, h, o = t.back(1), t.back(2), t.back(3), t.back(4)
                    if e.there():
                        act.wait_ge(qkT_done, 2 * e.done() - 1)
                        if e.back(1).there():
                            act.wait_ge(s_done, e.back(1).done(2))
                        nc.scalar.activation(qT[:, :], ps[:, 5, :], ACT.Copy).then_inc(qkT_in, 1)
                        act.wait_ge(qkT_done, e.done(2))
                        nc.scalar.activation(kT[:, :, e.slot * P:(e.slot + 1) * P],
                                             ps[:, 6, :].rearrange("p (i n) -> p i n", n=P), ACT.Copy).then_inc(qkT_in, 1)
                    if h.there():
                        exponentials(h, 1)
                    if b.there():
                        act.wait_ge(v_done, b.done())
                        if b.back(3).there():
                            act.wait_ge(pv_done, b.back(3).done())
                        nc.scalar.activation(va[:, b.slot, :, :], ps[:, 2, :].rearrange("p (h d) -> p h d", d=DH), ACT.Copy).then_inc(v_in, 1)
                    if o.there():
                        act.wait_ge(pv_done, o.done())
                        if o.back(1).there():
                            act.wait_ge(wo_done, o.back(1).done())
                        nc.scalar.activation(oT[:, :], ps[:, 7, :], ACT.Copy).then_inc(oT_in, 1)
                    if h.there():
                        fetch_pT(h, 0)
                    if t.there():
                        act.wait_ge(xT_done, t.done())
                        c = t.slot * P
                        both = ps[:, 2, 0:2 * P].rearrange("p (a n) -> p a n", a=2)
                        nc.scalar.activation(hT[0:64, :, c:c + P].bitcast(F32R), both[0:64], ACT.Copy)
                        nc.scalar.activation(hT[64:P, :, c + 1:c + P + 1].bitcast(F32R), both[64:P], ACT.Copy).then_inc(hT_ready, 1)
                    if e.there():
                        exponentials(e, 0)
                    if h.there():
                        fetch_pT(h, 1)
                    stage(t.back(-1))
                    if t.there():
                        act.wait_ge(qk_done, t.done())
                        if t.back(1).there():
                            act.wait_ge(ss_raw, t.back(1).done())
                        nc.scalar.activation(sq[:, :].rearrange("p (a n) -> p a n", a=2), ps[:, 0:2, :], ACT.Square).then_inc(squared, 1)

                stage(Tile(l, 0, 0))
                tile_steps(act, l, 4, step)

                act.wait_ge(x_attn, NT * (l + 1))
                load_attn(1 - l)
                act.wait_ge(ffn_w_in, 16 * N_FFN_W * (l + 1))
                nc.scalar.activation(w1_hl[:, 0, :].bitcast(F32R), w1_s[:, :], ACT.Copy).then_inc(w1_hi, 1)
                act.wait_ge(norm_ready, l + 1)

                def ffn(s, n):
                    g = l * SEQS + s

                    def gelu(c):
                        r = g - 2
                        act.wait_ge(w1_done, CH * r + c + 1)
                        rows = HC if c < CH - 1 else HL
                        if c >= 2 or past(n, 3):
                            act.wait_ge(u_ready, CH * r + c - 1)
                        nc.scalar.activation(gl[0:rows, c % 2, :], ps[0:rows, 3 + 2 * (c % 2), :], ACT.Gelu,
                                             bias=b1_s[0:rows, 1, c:c + 1]).then_inc(gelu_done, 1)

                    if on(n, 2):
                        gelu(0)
                        gelu(1)
                    if on(n, 1):
                        r = g - 1
                        if past(n, 2):
                            act.wait_ge(hnT_lo, r)
                        for part, dst, src in ((slice(64, P), slice(0, 1), norm0[64:P, bass.ds(s - 1, 1)]),
                                               (slice(0, 64), slice(0, SEQ), ps[0:64, 1, :]),
                                               (slice(64, P), slice(1, SEQ + 1), ps[64:P, 1, :])):
                            if dst.stop == SEQ:
                                act.wait_ge(hnT_done, r + 1)
                            last = nc.scalar.activation(hnT[part, dst], src, ACT.Identity,
                                                        bias=lgb_s[part, 1:2], scale=lgb_s[part, 0:1])
                        last.then_inc(hnT_in, 1)
                    if on(n, 2):
                        gelu(CH - 1)
                    if on(n, 1):
                        act.wait_ge(hnT_in, r + 1)
                        if past(n, 2):
                            act.wait_ge(w1_done, CH * r)
                        nc.scalar.activation(hnT_hl[:, 0, :].bitcast(F32R), hnT[:, 0:SEQ], ACT.Copy).then_inc(hnT_hi, 1)

                seq_steps(act, 2, ffn)

            act.wait_ge(attn_w_in, 16 * N_ATTN_W * (DEPTH + 1))
            act.wait_ge(e_nb, 1)
            with act.Fori(0, SEQS) as s:
                for i in range(TILES):
                    last = nc.scalar.activation(x1[:, s * TILES + i, :], x1[:, s * TILES + i, :], ACT.Identity,
                                                bias=e_tmp[:, 5, bass.ds(s * TILES + i, 1)])
                last.then_inc(e_bias, 1)

        @block.vector
        def _(dve):
            dve.wait_ge(setup_done, SETUPS)
            dve.wait_ge(consts_in, 16 * N_CONSTS)

            places = count()

            def take_wait():
                col = next(places) % WAITS
                nc.vector.memset(waited[:, col:col + 1], 0.0)

            def spread(k, src, st_sem, s):
                take_wait()
                for i in range(TILES):
                    nc.vector.bn_stats(stats[:, k, i, :], src(i)).then_inc(st_sem, 1)
                dve.wait_ge(st_sem, TILES * (s + 1))
                take_wait()
                for i in range(TILES):
                    last = nc.vector.bn_aggr(mv[:, k, i, :], stats[:, k, i, :])
                return last

            def ret(s, n):
                if on(n, 0):
                    dve.wait_ge(x_in, 16 * (s + 1))
                    last = spread(0, lambda i: x1[:, s * TILES + i, :], x_st, s)
                if on(n, 4):
                    r = s - 4
                    dve.wait_ge(x1_ready, r + 1)
                    last = spread(2, lambda i: x1[:, r * TILES + i, :], f_st, r)
                if on(n, 3):
                    r = s - 3
                    dve.wait_ge(ret_o_done, r + 1)
                    last = spread(1, lambda i: ps[:, 7, i * P:(i + 1) * P], o_st, r)
                if on(n, 0) or on(n, 4) or on(n, 3):
                    last.then_inc(var_ready, 1)
                dve.wait_ge(std_ready, s + 1)
                if past(n, 1):
                    if n is None or n <= SEQS:
                        dve.wait_ge(xn_ready, s)
                if past(n, 5):
                    dve.wait_ge(stream, s - 4)
                nc.vector.reciprocal(rstd[:, :, :], std[:, :, :]).then_inc(rstd_ready, 1)
                dve.wait_ge(rstd_ready, s + 1)
                nc.vector.scalar_tensor_tensor(out=nbias[:, :, :], in0=mv[:, :, :, 0], scalar=-1.0, in1=rstd[:, :, :],
                                               op0=ALU.mult, op1=ALU.mult).then_inc(scal_ready, 1)
                if on(n, 2):
                    r = s - 2
                    dve.wait_ge(ret_s_done, r + 1)
                    if past(n, 3):
                        dve.wait_ge(ret_o_done, r)
                    for j in range(TILES):
                        w = SEQ - j * P
                        src = ps[:, 4 + j, 0:w] if j < 3 else ps[:, 6, 2 * P:3 * P]
                        last = nc.vector.tensor_tensor(sT[:, j, 0:w], src, decay_s[:, 0:w], ALU.mult)
                    last.then_inc(decayed, 1)

            seq_steps(dve, 4, ret)

            with dve.Fori(0, DEPTH) as l:
                dve.wait_ge(stream, SEQS * (l + 1))
                dve.wait_ge(attn_w_in, 16 * N_ATTN_W * (l + 1))
                for w in range(2):
                    sc = qks_s[:, w, :].unsqueeze(1).to_broadcast([P, TILES, DH])
                    nc.vector.tensor_tensor(tab[:, :, 0, w, :], rot_s[:, :, 2 * w, :], sc, ALU.mult)
                    for a, b in ((0, 32), (32, 0)):
                        sc = qks_s[:, w, b:b + 32].unsqueeze(1).to_broadcast([P, TILES, 32])
                        last = nc.vector.tensor_tensor(tab[:, :, 1, w, a:a + 32], rot_s[:, :, 2 * w + 1, a:a + 32], sc, ALU.mult)
                last.then_inc(tab_ready, 1)
                dve.wait_ge(tab_ready, l + 1)

                def step(t):
                    h = t.back(3)

                    def invert(a):
                        if h.there():
                            dve.wait_ge(p_ready, 2 * h.done() - 1 + a)
                            if h.back(1).there():
                                dve.wait_ge(pn_ready, 2 * h.back(1).done() - 1 + a)
                            part = slice(a * PAIRS, (a + 1) * PAIRS)
                            nc.vector.reciprocal(rsum[:, part], psum_p[:, part]).then_inc(rsum_ready, 1)

                    def maxima(a):
                        if e.there():
                            dve.wait_ge(s_done, 2 * e.done() - 1 + a)
                            if e.back(1).there():
                                dve.wait_ge(p_ready, 2 * e.back(1).done() - 1 + a)
                            nc.vector.tensor_reduce(out=smax[:, a * PAIRS:(a + 1) * PAIRS],
                                                    in_=ps[:, 3 + a, :].rearrange("p (h c) -> p h c", c=P),
                                                    axis=AXX, op=ALU.max, negate=True).then_inc(smax_done, 1)

                    invert(0)
                    b = t.back(1)
                    e = t.back(2)
                    if b.there():
                        dve.wait_ge(squared, b.done())
                        nc.vector.tensor_reduce(out=ss[:, :], in_=sq[:, :].rearrange("p (h d) -> p h d", d=DH),
                                                axis=AXX, op=ALU.add).then_inc(ss_raw, 1)
                        if b.back(1).there():
                            dve.wait_ge(summed, b.back(1).done())
                        root = Newton(dve, nc, newt, b.back(1).done(NEWTON_STEPS), ss[:, :], nt_half[:, :], rn[:, :], nt_tmp[:, :])

                        def rotate(dst, k, w, to, frm, n):
                            return nc.vector.tensor_tensor(
                                dst[:, w, :].rearrange("p a (h d) -> p a h d", d=DH)[:, :, :, to:to + n],
                                ps[:, w, :].rearrange("p a (h d) -> p a h d", d=DH)[:, :, :, frm:frm + n],
                                tab[:, b.slot, k, w, to:to + n].unsqueeze(2).to_broadcast([P, w.stop - w.start, HEADS, n]), ALU.mult)

                        half = DH // 2
                        rotate(qk_c, 0, slice(0, 1), 0, 0, DH)
                        dve.wait_ge(ss_raw, b.done())
                        nc.vector.tensor_scalar(ss[:, :], ss[:, :], 1e-24, None, ALU.max).then_inc(ss_ready, 1)
                        rotate(qk_c, 0, slice(1, 2), 0, 0, DH)
                        dve.wait_ge(ss_ready, b.done())
                        root.seed()
                    invert(1)
                    if b.there():
                        rotate(qk_s, 1, slice(0, 2), 0, half, half)
                        if b.back(1).there():
                            dve.wait_ge(qk_ready, b.back(1).done(2))
                        root.guess()
                        rotate(qk_s, 1, slice(0, 2), half, 0, half).then_inc(rotated, 1)
                        root.square(0)
                    maxima(0)
                    if b.there():
                        root.times_v(0)
                        root.update(0)
                        for k in range(1, NEWTON):
                            root.square(k)
                            root.times_v(k)
                            root.update(k)
                    o = t.back(4)
                    if o.there():
                        dve.wait_ge(wo_done, o.done())
                        nc.vector.tensor_tensor(xf[:, o.n, :], xf[:, o.n, :], ps[:, 2, 2 * P:3 * P], ALU.add).then_inc(x_attn, 1)
                    maxima(1)
                    w = t.back(5)
                    if w.there():
                        dve.wait_ge(x_attn, w.done())
                        take_wait()
                        nc.vector.bn_stats(h_stats[:, 0, w.n, :], xf[:, w.n, 0:64])
                        nc.vector.bn_stats(h_stats[:, 1, w.n, :], xf[:, w.n, 64:P]).then_inc(h_st, 1)

                tile_steps(dve, l, 5, step)

                dve.wait_ge(h_st, NT * (l + 1))
                own = H_STEPS * l
                total, diff, var, half, y, tmp = (e_tmp[:, i, :] for i in range(6))
                nc.vector.tensor_tensor(h_mom[:, :, 0, :], h_stats[:, :, :, 1], h_stats[:, :, :, 4], ALU.add)
                nc.vector.tensor_tensor(h_mom[:, :, 1, :], h_stats[:, :, :, 2], h_stats[:, :, :, 5], ALU.add)
                nc.vector.tensor_tensor(h_diff[:, :, :], h_stats[:, :, :, 1], h_stats[:, :, :, 4], ALU.subtract).then_inc(h_step, 1)
                dve.wait_ge(h_step, own + 1)
                nc.vector.tensor_tensor(h_diff[:, :, :], h_diff[:, :, :], h_diff[:, :, :], ALU.mult).then_inc(h_step, 1)
                dve.wait_ge(h_step, own + 2)
                nc.vector.scalar_tensor_tensor(out=h_mom[:, :, 1, :], in0=h_diff[:, :, :], scalar=DIM / 8.0, in1=h_mom[:, :, 1, :],
                                               op0=ALU.mult, op1=ALU.add).then_inc(mom_ready, 1)
                dve.wait_ge(mom_moved, l + 1)
                dve.wait_ge(mom_ready, l + 1)
                moved = ps[:, 0, 0:2 * NT].rearrange("p (a n) -> p a n", a=2)
                nc.vector.tensor_tensor(total, h_mom[:, 0, 0, :], moved[:, 0, :], ALU.add)
                nc.vector.tensor_tensor(var, h_mom[:, 0, 1, :], moved[:, 1, :], ALU.add)
                nc.vector.tensor_tensor(diff, h_mom[:, 0, 0, :], moved[:, 0, :], ALU.subtract).then_inc(h_step, 1)
                dve.wait_ge(h_step, own + 3)
                nc.vector.tensor_tensor(diff, diff, diff, ALU.mult)
                nc.vector.tensor_scalar(var, var, 1.0 / DIM, EPS, ALU.mult, ALU.add).then_inc(h_step, 1)
                dve.wait_ge(h_step, own + 4)
                nc.vector.scalar_tensor_tensor(out=var, in0=diff, scalar=1.0 / 16, in1=var, op0=ALU.mult, op1=ALU.add).then_inc(h_step, 1)
                dve.wait_ge(h_step, own + 5)
                Newton(dve, nc, f_newt, NEWTON_STEPS * l, var, half, y, tmp).whole()
                dve.wait_ge(f_newt, NEWTON_STEPS * (l + 1))
                nc.vector.tensor_copy(norm[:, 0, :, 0], y)
                nc.vector.scalar_tensor_tensor(out=norm[:, 1, :, 0], in0=total, scalar=-0.25, in1=y,
                                               op0=ALU.mult, op1=ALU.mult).then_inc(norm_own, 1)
                dve.wait_ge(norm_moved, l + 1)
                nc.vector.tensor_copy(norm[:, :, :, 1], ps[:, 0, 0:2 * NT].rearrange("p (a n) -> p a n", a=2))
                nc.vector.tensor_copy(norm0[:, :], ps[:, 0, 2 * NT:2 * NT + SEQS]).then_inc(norm_ready, 1)

                dve.wait_ge(ffn_w_in, 16 * N_FFN_W * (l + 1))

                def ffn(s, n):
                    g = l * SEQS + s
                    if on(n, 2):
                        r = g - 2
                        for c in range(CH):
                            dve.wait_ge(gelu_done, CH * r + c + 1)
                            if past(n, 3):
                                dve.wait_ge(w2_done, r)
                            rows = HC if c < CH - 1 else HL
                            nc.vector.scalar_tensor_tensor(
                                out=u[0:rows, c, :], in0=ps[0:rows, 2 + 2 * (c % 2), :], scalar=b1_s[0:rows, 0, c:c + 1],
                                in1=gl[0:rows, c % 2, :], op0=ALU.add, op1=ALU.mult).then_inc(u_ready, 1)
                    if on(n, 1):
                        dve.wait_ge(hnT_hi, g)
                        nc.vector.tensor_tensor(hnT_hl[:, 1, :].bitcast(F32R), hnT[:, 0:SEQ], hnT_hl[:, 0, :],
                                                ALU.subtract).then_inc(hnT_lo, 1)
                    if on(n, 3):
                        dve.wait_ge(stream, SEQS + g - 2)
                        take_wait()
                        for i in range(TILES):
                            last = nc.vector.bn_stats(e_stats[:, (s - 3) * TILES + i, :], xf[:, (s - 3) * TILES + i, :])
                        last.then_inc(e_st, 1)
                    if on(n, 2):
                        r = g - 2
                        dve.wait_ge(w2_done, r + 1)
                        nc.vector.tensor_tensor(seq_rows(xf, s - 2), seq_rows(xf, s - 2),
                                                ps[:, 6, :].rearrange("p (t d) -> p t d", t=TILES), ALU.add).then_inc(stream, 1)

                seq_steps(dve, 3, ffn)

            dve.wait_ge(e_st, SEQS * DEPTH)
            m_even, m_odd = e_stats[:, :, 1], e_stats[:, :, 4]
            total, diff, var, half, y, nb = (e_tmp[:, i, :] for i in range(6))
            nc.vector.tensor_tensor(total, m_even, m_odd, ALU.add)
            nc.vector.tensor_tensor(var, e_stats[:, :, 2], e_stats[:, :, 5], ALU.add)
            nc.vector.tensor_tensor(diff, m_even, m_odd, ALU.subtract).then_inc(e_st, 1)
            dve.wait_ge(e_st, SEQS * DEPTH + 1)
            nc.vector.tensor_tensor(diff, diff, diff, ALU.mult)
            nc.vector.tensor_scalar(var, var, 1.0 / DIM, EPS, ALU.mult, ALU.add).then_inc(e_st, 1)
            dve.wait_ge(e_st, SEQS * DEPTH + 2)
            nc.vector.scalar_tensor_tensor(out=var, in0=diff, scalar=0.25, in1=var, op0=ALU.mult, op1=ALU.add).then_inc(e_st, 1)
            dve.wait_ge(e_st, SEQS * DEPTH + 3)
            Newton(dve, nc, e_newt, 0, var, half, y, diff).whole()
            dve.wait_ge(e_newt, NEWTON_STEPS)
            nc.vector.scalar_tensor_tensor(out=nb, in0=total, scalar=-0.5, in1=y, op0=ALU.mult, op1=ALU.mult).then_inc(e_nb, 1)
            with dve.Fori(0, SEQS) as s:
                dve.wait_ge(e_bias, s + 1)
                for i in range(TILES):
                    t = s * TILES + i
                    last = nc.vector.scalar_tensor_tensor(out=x1[:, t, :], in0=xf[:, t, :], scalar=e_tmp[:, 4, bass.ds(t, 1)],
                                                          in1=x1[:, t, :], op0=ALU.mult, op1=ALU.add)
                last.then_inc(e_sum, 1)

        @block.tensor
        def _(pe):
            pe.wait_ge(setup_done, SETUPS)
            pe.wait_ge(consts_in, 16 * N_CONSTS)
            pe.wait_ge(ret_w_in, 16 * N_RET_W)
            mm = nc.tensor.matmul

            def ret(s, n):
                if on(n, 2):
                    r = s - 2
                    pe.wait_ge(xnT_in, r + 1)
                    if past(n, 3):
                        pe.wait_ge(rqk_in, r)
                        pe.wait_ge(rv_in, r)
                    mm(ps[:, 1, :], wq_s[:, :], xnT[:, :], start=True, stop=True).then_inc(proj_done, 1)
                    mm(ps[:, 2, :], wk_s[:, :], xnT[:, :], start=True, stop=True).then_inc(proj_done, 1)
                    for i in range(TILES):
                        last = mm(ps[:, 3, i * P:(i + 1) * P], xnT[:, i * P:(i + 1) * P], wv_s[:, :], start=True, stop=True)
                    last.then_inc(proj_done, 1)
                if on(n, 3):
                    r = s - 3
                    pe.wait_ge(decayed, r + 1)
                    pe.wait_ge(rv_in, r + 1)
                    if past(n, 4):
                        pe.wait_ge(on_ready, r)
                    for i in range(TILES):
                        for j in range(i + 1):
                            last = mm(ps[:, 7, i * P:(i + 1) * P], sT[:, j, (i - j) * P:(i - j + 1) * P],
                                      rv[:, j * P:(j + 1) * P], start=(j == 0), stop=(j == i))
                    last.then_inc(ret_o_done, 1)
                if on(n, 1):
                    r = s - 1
                    pe.wait_ge(xn_ready, r + 1)
                    if past(n, 2):
                        pe.wait_ge(xnT_in, r)
                    for i in range(TILES):
                        last = nc.tensor.transpose(ps[:, 0, i * P:(i + 1) * P], xn[:, i, :], id_f[:, :])
                    last.then_inc(xnT_done, 1)
                if on(n, 2):
                    r = s - 2
                    pe.wait_ge(rqk_in, r + 1)
                    if past(n, 3):
                        pe.wait_ge(decayed, r)
                    for j in range(TILES):
                        w = SEQ - j * P
                        dst = ps[:, 4 + j, 0:w] if j < 3 else ps[:, 6, 2 * P:3 * P]
                        last = mm(dst, rk[:, j * P:(j + 1) * P], rq[:, j * P:SEQ], start=True, stop=True)
                    last.then_inc(ret_s_done, 1)

            seq_steps(pe, 4, ret)

            with pe.Fori(0, DEPTH) as l:
                pe.wait_ge(stream, SEQS * (l + 1))
                pe.wait_ge(attn_w_in, 16 * N_ATTN_W * (l + 1))
                pe.wait_ge(wqkv_lo, l + 1)

                def step(t):
                    d, b, h, o = t.back(2), t.back(1), t.back(3), t.back(4)
                    if b.there():
                        pe.wait_ge(hT_ready, b.done())
                        if b.back(1).there():
                            pe.wait_ge(rotated, b.back(1).done())
                            pe.wait_ge(squared, b.back(1).done())
                        c = b.slot * P
                        for banks, done in (((0, 1), qk_done), ((2,), v_done)):
                            if banks == (2,) and b.back(4).there():
                                pe.wait_ge(x_attn, b.back(4).done())
                            for x_part, w_part in ((0, 0), (0, 1), (1, 0)):
                                for w in banks:
                                    last = mm(ps[:, w, :], hT[:, x_part, c:c + P].bitcast(F32R),
                                              wqkv_hl[:, w_part, w * INNER:(w + 1) * INNER].bitcast(F32R),
                                              start=(x_part + w_part == 0), stop=(x_part == 1))
                            last.then_inc(done, 1)
                    if d.there():
                        for w in range(2):
                            pe.wait_ge(qk_ready, 2 * d.done() - 1 + w)
                            if d.back(2).there():
                                pe.wait_ge(pT_in, 2 * d.back(2).done() - 1 + w)
                            for i in range(PAIRS):
                                last = nc.tensor.transpose(ps[:, 5 + w, i * P:(i + 1) * P], qk[:, w, i * P:(i + 1) * P], id_f[:, :])
                            last.then_inc(qkT_done, 1)
                    if o.there():
                        pe.wait_ge(pT_in, o.done(2))
                        pe.wait_ge(vb_in[o.slot], (16 if o.slot == 0 else 32) * (o.layer * SEQS + o.batch + 1))
                        if o.back(1).there():
                            pe.wait_ge(oT_in, o.back(1).done())
                        for i in range(HEADS):
                            j, par = i % 2 * PAIRS + i // 2, i % 2
                            for half, values in enumerate((vb, va)):
                                q = slice(half * WIN, (half + 1) * WIN)
                                last = mm(ps[par * DH:(par + 1) * DH, 7, i // 2 * P + q.start:i // 2 * P + q.stop],
                                          values[:, o.slot, i, :], pT[:, j, q], start=True, stop=True)
                        last.then_inc(pv_done, 1)

                    def transpose_p(a):
                        if h.there():
                            if d.there():
                                pe.wait_ge(qkT_in, 2 * d.done() - 1 + a)
                            pe.wait_ge(pn_ready, 2 * h.done() - 1 + a)
                            for i in range(PAIRS):
                                last = nc.tensor.transpose(ps[:, 5 + a, i * P:(i + 1) * P], prob[:, a * PAIRS + i, :], id_f[:, :])
                            last.then_inc(pT_done, 1)

                    def scores(par):
                        if d.there():
                            if par == 0:
                                pe.wait_ge(qkT_in, d.done(2))
                            if d.back(1).there():
                                pe.wait_ge(p_ready, 2 * d.back(1).done() - 1 + par)
                            v = 1 if d.slot else 0
                            mm(ps[:, 3 + par, :], id_b[:, :], mask_b[:, v * 512:(v + 1) * 512], start=True, stop=False,
                               skip_group_check=True)
                            r = slice(par * DH, (par + 1) * DH)
                            for i in range(PAIRS):
                                for half in range(2):
                                    first = d.slot == 0 and half == 0
                                    lo = d.slot * P + (0 if first else (half - 1) * WIN)
                                    hi = d.slot * P + (half + 1) * WIN
                                    last = mm(ps[half * WIN:(half + 1) * WIN, 3 + par, (i + 1) * P - (hi - lo):(i + 1) * P],
                                              qT[r, i * P + half * WIN:i * P + (half + 1) * WIN], kT[r, i, lo:hi],
                                              start=False, stop=(i == PAIRS - 1), skip_group_check=True)
                            last.then_inc(s_done, 1)

                    transpose_p(0)
                    scores(0)
                    if t.there():
                        pe.wait_ge(x_lo, t.done())
                        if t.back(1).there():
                            pe.wait_ge(v_in, t.back(1).done())
                        nc.tensor.transpose(ps[:, 2, 0:P], xstage[:, t.slot % 2, 0, :], id_f[:, :])
                        nc.tensor.transpose(ps[:, 2, P:2 * P], xstage[:, t.slot % 2, 1, :], id_f[:, :]).then_inc(xT_done, 1)
                    scores(1)
                    transpose_p(1)
                    if o.there():
                        pe.wait_ge(oT_in, o.done())
                        if t.there():
                            pe.wait_ge(hT_ready, t.done())
                        elif b.there():
                            pe.wait_ge(v_in, b.done())
                        if o.back(1).there():
                            pe.wait_ge(x_attn, o.back(1).done())
                        for i in range(PAIRS):
                            last = mm(ps[:, 2, 2 * P:3 * P], oT[:, i * P:(i + 1) * P], wo_s[:, i, :], start=(i == 0), stop=(i == PAIRS - 1))
                        last.then_inc(wo_done, 1)


                tile_steps(pe, l, 4, step)

                by_tile = "p a (s t) -> p (a s) t"
                pe.wait_ge(mom_ready, l + 1)
                mm(ps[:, 0, 0:2 * NT], shift_s[:, 0, :], h_mom[:, 1, :, :].rearrange("p a n -> p (a n)"),
                   start=True, stop=False, skip_group_check=True)
                mm(ps[:, 0, 0:2 * NT].rearrange("p (s t) -> p s t", t=TILES)[:, :, 1:TILES], shift_s[:, 1, :],
                   h_mom[:, 1, :, :].rearrange(by_tile, t=TILES)[:, :, 0:TILES - 1],
                   start=False, stop=True, skip_group_check=True).then_inc(mom_moved, 1)
                pe.wait_ge(norm_own, l + 1)
                mm(ps[:, 0, 0:2 * NT], shift_s[:, 2, :], norm[:, :, :, 0].rearrange("p a n -> p (a n)"),
                   start=True, stop=False, skip_group_check=True)
                mm(ps[:, 0, 0:2 * NT].rearrange("p (s t) -> p s t", t=TILES)[:, :, 0:TILES - 1], shift_s[:, 3, :],
                   norm[:, :, :, 0].rearrange(by_tile, t=TILES)[:, :, 1:TILES],
                   start=False, stop=True, skip_group_check=True)
                mm(ps[:, 0, 2 * NT:2 * NT + SEQS], shift_s[:, 4, :],
                   norm[:, 1, :, 0].rearrange("p (s t) -> p s t", t=TILES)[:, :, 0],
                   start=True, stop=True).then_inc(norm_moved, 1)
                pe.wait_ge(w1_lo, l + 1)
                pe.wait_ge(ffn_w_in, 16 * N_FFN_W * (l + 1))

                def ffn(s, n):
                    g = l * SEQS + s

                    def w1_product(c):
                        r = g - 2
                        rows = HC if c < CH - 1 else HL
                        if c == 0:
                            pe.wait_ge(hnT_lo, r + 1)
                        if c >= 2 or past(n, 3):
                            pe.wait_ge(u_ready, CH * r + c - 1)
                        for h in range(2):
                            cols = slice(h * HID + c * HC, h * HID + c * HC + rows)
                            for w_part, x_part in ((0, 0), (0, 1), (1, 0)):
                                last = mm(ps[0:rows, 2 + 2 * (c % 2) + h, :], w1_hl[:, w_part, cols].bitcast(F32R),
                                          hnT_hl[:, x_part, :].bitcast(F32R), start=(w_part + x_part == 0), stop=(w_part == 1))
                        last.then_inc(w1_done, 1)

                    if on(n, 2):
                        w1_product(0)
                        w1_product(1)
                    if on(n, 1):
                        r = g - 1
                        pe.wait_ge(hn_ready, r + 1)
                        if past(n, 2):
                            pe.wait_ge(hnT_in, r)
                        for i in range(TILES):
                            last = nc.tensor.transpose(ps[:, 1, i * P:(i + 1) * P], hn[:, i, :], id_f[:, :])
                        last.then_inc(hnT_done, 1)
                    if on(n, 2):
                        w1_product(2)
                        r = g - 2
                        if past(n, 3):
                            pe.wait_ge(stream, SEQS + r)
                        for c in range(CH):
                            pe.wait_ge(u_ready, CH * r + c + 1)
                            for i in range(TILES):
                                last = mm(ps[:, 6, i * P:(i + 1) * P], u[0:HC, c, i * P:(i + 1) * P], w2_s[:, c, :],
                                          start=(c == 0 and i == 0), stop=(c == CH - 1), skip_group_check=True)
                        last.then_inc(w2_done, 1)

                seq_steps(pe, 2, ffn)


def kernel(L0_attn_x, L0_attn_Wq, L0_attn_bq, L0_attn_Wk, L0_attn_bk, L0_attn_Wv, L0_ffn_wqkv, L0_ffn_q_scale,
           L0_ffn_k_scale, L0_ffn_wo, L0_ffn_ln_g, L0_ffn_ln_b, L0_ffn_w1, L0_ffn_b1, L0_ffn_w2, L0_ffn_b2):
    import concourse.bacc as bacc
    from concourse.bass_utils import run_bass_kernel_spmd

    a = np.asarray
    b1 = np.zeros((DEPTH, 2, CH * HC), np.float32)
    b1[:, :, 0:HID] = a(L0_ffn_b1).reshape(DEPTH, 2, HID)
    w2 = np.concatenate([a(L0_ffn_w2), a(L0_ffn_b2)[:, None, :]], axis=1)
    qks = np.stack([a(L0_ffn_q_scale), a(L0_ffn_k_scale)], axis=1)
    arrays = {
        "x": a(L0_attn_x).reshape(SEQS * SEQ, DIM),
        "wq": a(L0_attn_Wq).T, "wk": a(L0_attn_Wk).T, "wv": a(L0_attn_Wv).T,
        "bqk": np.stack([a(L0_attn_bq), a(L0_attn_bk)], axis=1),
        "wqkv": a(L0_ffn_wqkv),
        "qks": np.broadcast_to(qks[:, None], (DEPTH, P, 2, DH)),
        "wo": a(L0_ffn_wo),
        "lgb": np.stack([a(L0_ffn_ln_g), a(L0_ffn_ln_b)], axis=2),
        "w1": a(L0_ffn_w1),
        "b1": b1.reshape(DEPTH, 2, CH, HC).transpose(0, 3, 1, 2),
        "w2": w2.reshape(DEPTH, CH, HC, P).transpose(0, 2, 1, 3),
        **shape_constants(),
    }
    nc = bacc.Bacc("TRN2", target_bir_lowering=False, num_devices=1)
    args, sent = [], {}
    for name, v in arrays.items():
        v = np.ascontiguousarray(v)
        sent[f"in_{name}_dram"] = v
        args.append(nc.dram_tensor(f"in_{name}_dram", v.shape, mybir.dt.from_np(v.dtype), kind="ExternalInput").ap())
    args.append(nc.dram_tensor("out_0_dram", (SEQS * SEQ, DIM), F32, kind="ExternalOutput").ap())
    build(nc, *args)
    r = run_bass_kernel_spmd(nc, [sent], core_ids=[0])
    return r.results[0]["out_0_dram"].reshape(SEQS, SEQ, DIM)
```

```python
from contextlib import ExitStack
from itertools import count

import numpy as np

import concourse.bass as bass
from concourse import mybir

F32 = mybir.dt.float32
BF16 = mybir.dt.bfloat16
F32R = mybir.dt.float32r
I32 = mybir.dt.int32
ALU = mybir.AluOpType
ACT = mybir.ActivationFunctionType
AXX = mybir.AxisListType.X

P = 128
SEQS, SEQ, DIM = 16, 512, 128
TILES = SEQ // P
NT = SEQS * TILES
DEPTH, HEADS, DH, WIN = 2, 8, 64, 64
INNER = HEADS * DH
PAIRS = HEADS // 2
HID = DIM * 4 * 2 // 3
CH = 3
HC = (HID + CH) // CH
HL = HID - (CH - 1) * HC
GAMMA = 0.96875
EPS = 1e-5
MASKED = -1e30
RSQRT_SEED = float(0x5F3759DF)
NEWTON = 3
NEWTON_STEPS = 3 + 3 * NEWTON
E_GROUP = 4
WAITS = 16


def shape_constants():
    p = np.arange(P)
    ident = np.eye(P, dtype=np.float32)
    shift = np.zeros((P, 5, P), np.float32)
    shift[p[:-1], 0, p[1:]] = 1.0
    shift[P - 1, 1, 0] = 1.0
    shift[p[1:], 2, p[:-1]] = 1.0
    shift[0, 3, P - 1] = 1.0
    shift[0, 4, :] = 1.0
    c = np.arange(SEQ)
    e = (c[None, :] - p[:, None]).astype(np.float32)
    decay = np.where(e >= 0, np.power(np.float32(GAMMA), np.maximum(e, 0)), 0).astype(np.float32)
    half = np.arange(0, DH, 2, dtype=np.float32)
    inv_freq = (np.float32(1.0) / np.power(np.float32(10000.0), half / np.float32(DH))).astype(np.float32)
    t = np.arange(SEQ, dtype=np.float32)
    freqs = np.concatenate([t[:, None] * inv_freq[None, :]] * 2, axis=-1).astype(np.float32)
    base = ((half + np.float32(0.4 * DH)) / np.float32(1.4 * DH)).astype(np.float32)
    power = ((t - SEQ // 2) / np.float32(WIN // 2)).astype(np.float32)
    scale = np.power(base[None, :], power[:, None]).astype(np.float32)
    scale = np.concatenate([scale, scale], axis=-1)
    cos, sin = np.cos(freqs), np.sin(freqs)
    sign = np.where(np.arange(DH) < DH // 2, -1.0, 1.0).astype(np.float32)
    rot = np.stack([8.0 * cos * scale, 8.0 * sin * sign * scale, cos / scale, sin * sign / scale])
    rot = rot.reshape(4, TILES, P, DH).transpose(2, 1, 0, 3)
    q = np.arange(P)[:, None] % WIN
    k = np.arange(WIN)[None, :]
    ok = np.zeros((2, P, P), bool)
    ok[:, :, :WIN] = k >= q
    ok[:, :, WIN:] = k <= q
    ok[0, :WIN, :WIN] = False
    mask = np.where(ok, 0.0, MASKED).astype(np.float32)
    mask = np.tile(mask, (1, 1, 4)).transpose(1, 0, 2)
    return {
        "ident": ident, "shift": shift.reshape(P, 5 * P), "decay": decay,
        "rot": np.ascontiguousarray(rot.reshape(P, TILES * 4 * DH), dtype=np.float32),
        "mask": np.ascontiguousarray(mask.reshape(P, 8 * P)),
    }


class Tile:

    def __init__(self, layer, batch, j):
        self.layer, self.batch, self.slot = layer, batch + j // TILES, j % TILES
        self.n = self.batch * TILES + self.slot

    def back(self, k):
        return Tile(self.layer, self.batch, self.slot - k)

    def there(self):
        return not isinstance(self.n, int) or 0 <= self.n < NT

    def at(self, n):
        return isinstance(self.n, int) and self.n == n

    def done(self, per=1):
        return (self.layer * NT + self.n + 1) * per


def tile_steps(eng, layer, lag, body):
    for j in range(TILES + 1):
        body(Tile(layer, 0, j))
    with eng.Fori(1, SEQS - 1) as b:
        for j in range(1, TILES + 1):
            body(Tile(layer, b, j))
    for j in range(1, TILES + lag):
        body(Tile(layer, SEQS - 1, j))


def seq_steps(eng, lag, body):
    for s in range(lag + 1):
        body(s, s)
    with eng.Fori(lag + 1, SEQS) as s:
        body(s, None)
    for s in range(SEQS, SEQS + lag):
        body(s, s)


def on(n, back):
    return n is None or 0 <= n - back < SEQS


def past(n, back):
    return n is None or n - back >= 0


class Newton:

    def __init__(self, dve, nc, sem, base, v, half, y, tmp):
        self.dve, self.nc, self.sem, self.base = dve, nc, sem, base
        self.v, self.half, self.y, self.tmp = v, half, y, tmp

    def seed(self):
        v = self.nc.vector
        v.tensor_scalar(self.half, self.v, -0.5, None, ALU.mult).then_inc(self.sem, 1)
        v.tensor_scalar(self.tmp.bitcast(I32), self.v.bitcast(I32), 1, None, ALU.logical_shift_right).then_inc(self.sem, 1)

    def guess(self):
        self.dve.wait_ge(self.sem, self.base + 2)
        self.nc.vector.tensor_scalar(self.y.bitcast(I32), self.tmp.bitcast(I32), -1.0, RSQRT_SEED,
                                     ALU.mult, ALU.add).then_inc(self.sem, 1)

    def square(self, k):
        self.dve.wait_ge(self.sem, self.base + 3 + 3 * k)
        self.nc.vector.tensor_tensor(self.tmp, self.y, self.y, ALU.mult).then_inc(self.sem, 1)

    def times_v(self, k):
        self.dve.wait_ge(self.sem, self.base + 4 + 3 * k)
        self.nc.vector.tensor_tensor(self.tmp, self.tmp, self.half, ALU.mult).then_inc(self.sem, 1)

    def update(self, k):
        self.dve.wait_ge(self.sem, self.base + 5 + 3 * k)
        self.nc.vector.scalar_tensor_tensor(out=self.y, in0=self.tmp, scalar=1.5, in1=self.y,
                                            op0=ALU.add, op1=ALU.mult).then_inc(self.sem, 1)

    def whole(self):
        self.seed()
        self.guess()
        for k in range(NEWTON):
            self.square(k)
            self.times_v(k)
            self.update(k)


def build(nc, x, wq, wk, wv, bqk, wqkv, qks, wo, lgb, w1, b1, w2, ident, shift, decay, rot, mask, out):
    with ExitStack() as ctx:
        def sb(name, shape, dt=F32):
            return ctx.enter_context(nc.sbuf_tensor(name, shape, dt))

        def sem(name):
            return ctx.enter_context(nc.semaphore(name))

        x1 = sb("x1", [P, NT, DIM])
        xf = sb("xf", [P, NT, DIM])
        id_f = sb("id_f", [P, P])
        id_b = sb("id_b", [P, P], BF16)
        shift_s = sb("shift_s", [P, 5, P])
        decay_s = sb("decay_s", [P, SEQ])
        rot_s = sb("rot_s", [P, TILES, 4, DH])
        mask_b = sb("mask_b", [P, 8 * P], BF16)
        wq_s, wk_s, wv_s = sb("wq_s", [P, P]), sb("wk_s", [P, P]), sb("wv_s", [P, P])
        bqk_s = sb("bqk_s", [P, 2])
        eps_s = sb("eps_s", [P, 1])
        stats = sb("stats", [P, 3, TILES, 6])
        e_tmp = sb("e_tmp", [P, 6, NT])
        mv = sb("mv", [P, 3, TILES, 2])
        std = sb("std", [P, 3, TILES])
        rstd = sb("rstd", [P, 3, TILES])
        nbias = sb("nbias", [P, 3, TILES])
        xn = sb("xn", [P, TILES, P])
        xnT = sb("xnT", [P, SEQ])
        rq, rk, rv = sb("rq", [P, SEQ]), sb("rk", [P, SEQ]), sb("rv", [P, SEQ])
        on_s = sb("on_s", [P, TILES, P])
        wqkv_s = sb("wqkv_s", [P, 3 * INNER])
        wqkv_hl = sb("wqkv_hl", [P, 2, 3 * INNER])
        wo_s = sb("wo_s", [P, INNER // P, P])
        qks_s = sb("qks_s", [P, 2, DH])
        tab = sb("tab", [P, TILES, 2, 2, DH])
        xstage = sb("xstage", [P, 2, 2, P])
        hT = sb("hT", [P, 2, SEQ + 1])
        sq = sb("sq", [P, 2 * INNER])
        ss = sb("ss", [P, 16])
        rn = sb("rn", [P, 16])
        nt_half, nt_tmp = sb("nt_half", [P, 16]), sb("nt_tmp", [P, 16])
        sT = sb("sT", [P, TILES, SEQ])
        qk_c, qk_s = sT[:, 0:2, :], sT[:, 2:4, :]
        qk_sum = sb("qk_sum", [P, 2, INNER])
        qk = sb("qk", [P, 2, INNER])
        qT = sb("qT", [P, INNER])
        kT = sb("kT", [P, PAIRS, SEQ])
        smax = sb("smax", [P, HEADS])
        prob = sb("prob", [P, HEADS, P])
        mask_f = prob[:, :, :].rearrange("p h c -> p (h c)")
        pT = sb("pT", [P, HEADS, P])
        va = sb("va", [P, TILES, HEADS, DH])
        vb = sb("vb", [P, TILES, HEADS, DH])
        psum_p, rsum = sb("psum_p", [P, HEADS]), sb("rsum", [P, HEADS])
        oT = sb("oT", [P, INNER])
        waited = sb("waited", [P, WAITS])
        w1_s = sb("w1_s", [P, 2 * HID])
        w1_hl = sb("w1_hl", [P, 2, 2 * HID])
        w2_s = sb("w2_s", [HC, CH, P])
        b1_s = sb("b1_s", [HC, 2, CH])
        lgb_s = sb("lgb_s", [P, 2])
        h_stats = sb("h_stats", [P, 2, NT, 6])
        e_stats = h_stats[:, 0]
        h_mom = sb("h_mom", [P, 2, 2, NT])
        h_diff = sb("h_diff", [P, 2, NT])
        norm = sb("norm", [P, 2, NT, 2])
        norm0 = sb("norm0", [P, SEQS])
        hn = xn
        hnT = sb("hnT", [P, SEQ + 1])
        hnT_hl = sb("hnT_hl", [P, 2, SEQ])
        gl = qk[0:HC]
        u = sb("u", [P, CH, SEQ])

        ps = ctx.enter_context(nc.psum_tensor("ps", [P, 8, 512], F32))

        consts_in, tables_in, ret_w_in, x_in = sem("consts_in"), sem("tables_in"), sem("ret_w_in"), sem("x_in")
        setup_done, bf16_ready = sem("setup_done"), sem("bf16_ready")
        x_st, o_st, f_st = sem("x_st"), sem("o_st"), sem("f_st")
        var_ready, std_ready, rstd_ready, scal_ready = (sem(n) for n in ("var_ready", "std_ready", "rstd_ready", "scal_ready"))
        x_scaled, xn_ready = sem("x_scaled"), sem("xn_ready")
        xnT_done, xnT_in = sem("xnT_done"), sem("xnT_in")
        proj_done, rqk_in, rv_in = sem("proj_done"), sem("rqk_in"), sem("rv_in")
        ret_s_done, decayed, ret_o_done = sem("ret_s_done"), sem("decayed"), sem("ret_o_done")
        on_ready, x1_ready = sem("on_ready"), sem("x1_ready")
        stream = sem("stream")
        attn_w_in, ffn_w_in = sem("attn_w_in"), sem("ffn_w_in")
        tab_ready = sem("tab_ready")
        wqkv_hi, wqkv_lo = sem("wqkv_hi"), sem("wqkv_lo")
        xstaged, x_lo, xT_done, hT_ready = sem("xstaged"), sem("x_lo"), sem("xT_done"), sem("hT_ready")
        qk_done, v_done, squared, v_in = sem("qk_done"), sem("v_done"), sem("squared"), sem("v_in")
        vb_in = [sem(f"vb_in{j}") for j in range(TILES)]
        rotated, summed, ss_raw, ss_ready, newt = (sem(n) for n in ("rotated", "summed", "ss_raw", "ss_ready", "newt"))
        qk_ready, qkT_done, qkT_in = sem("qk_ready"), sem("qkT_done"), sem("qkT_in")
        s_done, smax_done, p_ready = sem("s_done"), sem("smax_done"), sem("p_ready")
        pT_done, pT_in, pv_done = sem("pT_done"), sem("pT_in"), sem("pv_done")
        rsum_ready, pn_ready, oT_in = sem("rsum_ready"), sem("pn_ready"), sem("oT_in")
        wo_done, x_attn = sem("wo_done"), sem("x_attn")
        h_st, h_step, mom_ready, mom_moved = sem("h_st"), sem("h_step"), sem("mom_ready"), sem("mom_moved")
        f_newt, norm_own, norm_moved, norm_ready = sem("f_newt"), sem("norm_own"), sem("norm_moved"), sem("norm_ready")
        w1_hi, w1_lo, hn_scaled = sem("w1_hi"), sem("w1_lo"), sem("hn_scaled")
        hn_ready, hnT_done, hnT_in = sem("hn_ready"), sem("hnT_done"), sem("hnT_in")
        hnT_hi, hnT_lo = sem("hnT_hi"), sem("hnT_lo")
        w1_done, gelu_done, u_ready, w2_done = sem("w1_done"), sem("gelu_done"), sem("u_ready"), sem("w2_done")
        e_st, e_newt, e_nb, e_bias, e_own, e_sum, e_pool, stored = (sem(n) for n in ("e_st", "e_newt", "e_nb", "e_bias", "e_own", "e_sum", "e_pool", "stored"))

        N_CONSTS, N_TABLES, N_RET_W, N_ATTN_W, N_FFN_W = 2, 3, 4, 3, 4
        SETUPS = 5
        H_STEPS = 5
        PARTS = ((0, SEQS - 1), (SEQS - 1, SEQS))

        def seq_rows(t, s):
            return t[:, bass.ds(s * TILES, TILES), :]

        x_v = x.rearrange("(b t p) d -> b p t d", t=TILES, p=P)
        out_v = out.rearrange("(b t p) d -> b p t d", t=TILES, p=P)

        block = ctx.enter_context(nc.Block())

        @block.sync
        def _(sp):
            for s in range(SEQS):
                if s:
                    sp.wait_ge(x_in, 16 * s)
                nc.sync.dma_start(seq_rows(x1, s), x_v[s]).then_inc(x_in, 16)
                if s == 1:
                    nc.sync.dma_start(wqkv_s[:, :], wqkv[0]).then_inc(attn_w_in, 16)
                    nc.sync.dma_start(wo_s[:, :, :], wo[0].rearrange("(c p) n -> p c n", p=P)).then_inc(attn_w_in, 16)
                    nc.sync.dma_start(qks_s[:, :, :], qks[0]).then_inc(attn_w_in, 16)
                    nc.sync.dma_start(shift_s[:, :, :], shift.rearrange("p (a n) -> p a n", a=5)).then_inc(tables_in, 16)
                    nc.sync.dma_start(rot_s[:, :, :, :], rot.rearrange("p (t a d) -> p t a d", t=TILES, a=4)).then_inc(tables_in, 16)
                    nc.sync.dma_start(mask_f, mask).then_inc(tables_in, 16)

            with sp.Fori(0, DEPTH) as l:
                def step(t):
                    if t.there():
                        sp.wait_ge(v_in, t.done())
                        nc.sync.dma_start(vb[WIN:P, t.slot], va[0:WIN, t.slot]).then_inc(vb_in[t.slot], 16)
                        if t.slot < TILES - 1:
                            nc.sync.dma_start(vb[0:WIN, t.slot + 1], va[WIN:P, t.slot]).then_inc(vb_in[t.slot + 1], 16)

                tile_steps(sp, l, 0, step)

            for s in range(SEQS):
                k, m = divmod(s, E_GROUP)
                if m < E_GROUP - 1:
                    sp.wait_ge(e_sum, k * (E_GROUP - 1) + m + 1)
                else:
                    sp.wait_ge(e_pool, k + 1)
                nc.sync.dma_start(out_v[s], seq_rows(x1, s)).then_inc(stored, 16)
            sp.wait_ge(stored, 16 * SEQS)

        @block.gpsimd
        def _(pool):
            for i, (part, value) in enumerate((
                (hT[:, :, 0:1], 0.0),
                (vb[0:WIN, 0], 0.0),
                (u[96:P, CH - 1, :], 1.0),
                (eps_s[:, :], EPS),
                (mv[:, :, :, :], 1.0),
            )):
                nc.gpsimd.memset(part, value).then_inc(setup_done, 1)
                pool.wait_ge(setup_done, i + 1)

            def split_wqkv(n):
                pool.wait_ge(wqkv_hi, n)
                nc.gpsimd.tensor_tensor(wqkv_hl[:, 1, :].bitcast(F32R), wqkv_s[:, :], wqkv_hl[:, 0, :],
                                        ALU.subtract).then_inc(wqkv_lo, 1)

            def ret(s, n):
                if n == 4:
                    split_wqkv(1)
                if on(n, 0):
                    pool.wait_ge(scal_ready, s + 1)
                    if past(n, 1):
                        pool.wait_ge(xnT_done, s)
                    nc.gpsimd.tensor_tensor(xn[:, :, :], seq_rows(x1, s), rstd[:, 0, :].unsqueeze(2).to_broadcast([P, TILES, P]),
                                            ALU.mult).then_inc(x_scaled, 1)
                    pool.wait_ge(x_scaled, s + 1)
                    nc.gpsimd.tensor_tensor(xn[:, :, :], xn[:, :, :], nbias[:, 0, :].unsqueeze(2).to_broadcast([P, TILES, P]),
                                            ALU.add).then_inc(xn_ready, 1)
                if on(n, 3):
                    r = s - 3
                    pool.wait_ge(on_ready, r + 1)
                    nc.gpsimd.tensor_tensor(seq_rows(x1, r), seq_rows(x1, r), on_s[:, :, :], ALU.add).then_inc(x1_ready, 1)

            seq_steps(pool, 4, ret)

            with pool.Fori(0, DEPTH) as l:
                def split(t):
                    if t.there():
                        pool.wait_ge(xstaged, t.done())
                        nc.gpsimd.tensor_tensor(xstage[:, t.slot % 2, 1, :], xf[:, t.n, :], xstage[:, t.slot % 2, 0, :],
                                                ALU.subtract).then_inc(x_lo, 1)

                def step(t):
                    following = t.back(-1)
                    h = t.back(3)
                    if h.there():
                        for a in range(2):
                            pool.wait_ge(rsum_ready, 2 * h.done() - 1 + a)
                            part = prob[:, a * PAIRS:(a + 1) * PAIRS, :]
                            nc.gpsimd.tensor_tensor(part, part, rsum[:, a * PAIRS:(a + 1) * PAIRS].unsqueeze(2).to_broadcast(
                                [P, PAIRS, P]), ALU.mult).then_inc(pn_ready, 1)
                    t = t.back(1)
                    if t.there():
                        pool.wait_ge(rotated, t.done())
                        if t.back(1).there():
                            pool.wait_ge(qk_ready, t.back(1).done(2))
                        nc.gpsimd.tensor_tensor(qk_sum[:, :, :], qk_c[:, :, :], qk_s[:, :, :], ALU.add).then_inc(summed, 1)
                        pool.wait_ge(summed, t.done())
                        pool.wait_ge(newt, t.done(NEWTON_STEPS))
                        if t.back(1).there():
                            pool.wait_ge(qkT_done, t.back(1).done(2))
                        for w in range(2):
                            nc.gpsimd.tensor_tensor(
                                qk[:, w, :].rearrange("p (h d) -> p h d", d=DH),
                                qk_sum[:, w, :].rearrange("p (h d) -> p h d", d=DH),
                                rn[:, w * HEADS:(w + 1) * HEADS].unsqueeze(2).to_broadcast([P, HEADS, DH]), ALU.mult).then_inc(qk_ready, 1)
                    split(following)

                split(Tile(l, 0, 0))
                tile_steps(pool, l, 3, step)

                def ffn(s, n):
                    g = l * SEQS + s
                    if not on(n, 0):
                        return
                    xs = seq_rows(xf, s).rearrange("p t (a d) -> p (t a) d", a=2)
                    hs = hn[:, :, :].rearrange("p t (a d) -> p (t a) d", a=2)

                    def scalars(k):
                        return norm[:, k, bass.ds(s * TILES, TILES), :].rearrange("p t a -> p (t a)").unsqueeze(2).to_broadcast(
                            [P, 2 * TILES, DIM // 2])

                    if n == 0:
                        pool.wait_ge(norm_ready, 2 * l + 1)
                    if n == 1:
                        pool.wait_ge(w1_hi, l + 1)
                        nc.gpsimd.tensor_tensor(w1_hl[:, 1, :].bitcast(F32R), w1_s[:, :], w1_hl[:, 0, :],
                                                ALU.subtract).then_inc(w1_lo, 1)
                    if n == 3:
                        pool.wait_ge(norm_ready, 2 * l + 2)
                    if past(n, 1):
                        pool.wait_ge(hnT_done, g)
                    nc.gpsimd.tensor_tensor(hs, xs, scalars(0), ALU.mult).then_inc(hn_scaled, 1)
                    pool.wait_ge(hn_scaled, g + 1)
                    nc.gpsimd.tensor_tensor(hs, hs, scalars(1), ALU.add).then_inc(hn_ready, 1)

                seq_steps(pool, 3, ffn)
                split_wqkv(l + 2)

            pool.wait_ge(e_nb, 1)
            with pool.Fori(0, SEQS // E_GROUP) as k:
                s = k * E_GROUP + E_GROUP - 1

                def scalars(i):
                    return e_tmp[:, i, bass.ds(s * TILES, TILES)].unsqueeze(2).to_broadcast([P, TILES, DIM])

                nc.gpsimd.tensor_tensor(seq_rows(xf, s), seq_rows(xf, s), scalars(4), ALU.mult).then_inc(e_own, 1)
                pool.wait_ge(e_own, 2 * k + 1)
                nc.gpsimd.tensor_tensor(seq_rows(xf, s), seq_rows(xf, s), scalars(5), ALU.add).then_inc(e_own, 1)
                pool.wait_ge(e_own, 2 * k + 2)
                nc.gpsimd.tensor_tensor(seq_rows(x1, s), seq_rows(x1, s), seq_rows(xf, s), ALU.add).then_inc(e_pool, 1)

        @block.scalar
        def _(act):
            nc.scalar.dma_start(wq_s[:, :], wq).then_inc(ret_w_in, 16)
            nc.scalar.dma_start(wk_s[:, :], wk).then_inc(ret_w_in, 16)
            nc.scalar.dma_start(wv_s[:, :], wv).then_inc(ret_w_in, 16)
            nc.scalar.dma_start(bqk_s[:, :], bqk).then_inc(ret_w_in, 16)
            nc.scalar.dma_start(id_f[:, :], ident).then_inc(consts_in, 16)
            nc.scalar.dma_start(decay_s[:, :], decay).then_inc(consts_in, 16)

            def load_attn(l):
                nc.scalar.dma_start(wqkv_s[:, :], wqkv[l]).then_inc(attn_w_in, 16)
                nc.scalar.dma_start(wo_s[:, :, :], wo[l].rearrange("(c p) n -> p c n", p=P)).then_inc(attn_w_in, 16)
                nc.scalar.dma_start(qks_s[:, :, :], qks[l]).then_inc(attn_w_in, 16)

            def load_ffn(l):
                nc.scalar.dma_start(w1_s[:, :], w1[l]).then_inc(ffn_w_in, 16)
                nc.scalar.dma_start(w2_s[:, :, :], w2[l]).then_inc(ffn_w_in, 16)
                nc.scalar.dma_start(b1_s[:, :, :], b1[l]).then_inc(ffn_w_in, 16)
                nc.scalar.dma_start(lgb_s[:, :], lgb[l]).then_inc(ffn_w_in, 16)

            act.wait_ge(ret_w_in, 16 * N_RET_W)
            act.wait_ge(setup_done, SETUPS)

            def split_wqkv(n):
                act.wait_ge(attn_w_in, 16 * N_ATTN_W * n)
                nc.scalar.activation(wqkv_hl[:, 0, :].bitcast(F32R), wqkv_s[:, :], ACT.Copy).then_inc(wqkv_hi, 1)

            def normalise(dst, src, k):
                for i in range(TILES):
                    last = nc.scalar.activation(dst(i), src(i), ACT.Identity,
                                                bias=nbias[:, k, i:i + 1], scale=rstd[:, k, i:i + 1])
                return last

            def ret(s, n):
                if n == 3:
                    split_wqkv(1)
                if on(n, 2):
                    r = s - 2
                    act.wait_ge(proj_done, 3 * r + 2)
                    if past(n, 3):
                        act.wait_ge(ret_s_done, r)
                    nc.scalar.activation(rq[:, :], ps[:, 1, :], ACT.Identity, bias=bqk_s[:, 0:1])
                    nc.scalar.activation(rk[:, :], ps[:, 2, :], ACT.Identity, bias=bqk_s[:, 1:2]).then_inc(rqk_in, 1)
                if on(n, 1):
                    r = s - 1
                    act.wait_ge(xnT_done, r + 1)
                    if past(n, 2):
                        act.wait_ge(proj_done, 3 * r)
                    nc.scalar.activation(xnT[:, :], ps[:, 0, :], ACT.Copy).then_inc(xnT_in, 1)
                if on(n, 2):
                    r = s - 2
                    act.wait_ge(proj_done, 3 * r + 3)
                    if past(n, 3):
                        act.wait_ge(ret_o_done, r)
                    nc.scalar.activation(rv[:, :], ps[:, 3, :], ACT.Copy).then_inc(rv_in, 1)
                act.wait_ge(var_ready, s + 1)
                nc.scalar.activation(std[:, :, :], mv[:, :, :, 1], ACT.Sqrt, bias=eps_s[:, 0:1]).then_inc(std_ready, 1)
                act.wait_ge(scal_ready, s + 1)
                if on(n, 3):
                    r = s - 3
                    if past(n, 4):
                        act.wait_ge(x1_ready, r)
                    normalise(lambda i: on_s[:, i, :], lambda i: ps[:, 7, i * P:(i + 1) * P], 1).then_inc(on_ready, 1)
                if on(n, 4):
                    r = s - 4
                    normalise(lambda i: xf[:, r * TILES + i, :], lambda i: x1[:, r * TILES + i, :], 2).then_inc(stream, 1)

            seq_steps(act, 4, ret)

            act.wait_ge(bf16_ready, 2)
            with act.Fori(0, DEPTH) as l:
                act.wait_ge(stream, SEQS * (l + 1) - 1)

                def exponentials(t, a):
                    act.wait_ge(smax_done, 2 * t.done() - 1 + a)
                    if t.back(1).there():
                        act.wait_ge(pT_done, 2 * t.back(1).done() - 1 + a)
                    for i in range(PAIRS):
                        j = a * PAIRS + i
                        last = nc.scalar.activation(prob[:, j, :], ps[:, 3 + a, i * P:(i + 1) * P], ACT.Exp,
                                                    bias=smax[:, j:j + 1], accum_out=psum_p[:, j:j + 1])
                    last.then_inc(p_ready, 1)

                def fetch_pT(t, a):
                    act.wait_ge(pT_done, 2 * t.done() - 1 + a)
                    if t.back(1).there():
                        act.wait_ge(pv_done, t.back(1).done())
                    nc.scalar.activation(pT[:, a * PAIRS:(a + 1) * PAIRS, :], ps[:, 5 + a, :].rearrange("p (h q) -> p h q", q=P),
                                         ACT.Copy).then_inc(pT_in, 1)

                def stage(t):
                    if t.there():
                        if t.back(2).there():
                            act.wait_ge(xT_done, t.back(2).done())
                        nc.scalar.activation(xstage[:, t.slot % 2, 0, :].bitcast(F32R), xf[:, t.n, :], ACT.Copy).then_inc(xstaged, 1)

                def step(t):
                    b, e, h, o = t.back(1), t.back(2), t.back(3), t.back(4)
                    if t.at(2):
                        act.wait_ge(stream, SEQS * (l + 1))
                        load_ffn(l)
                    if e.there():
                        act.wait_ge(qkT_done, 2 * e.done() - 1)
                        if e.back(1).there():
                            act.wait_ge(s_done, e.back(1).done(2))
                        nc.scalar.activation(qT[:, :], ps[:, 5, :], ACT.Copy).then_inc(qkT_in, 1)
                        act.wait_ge(qkT_done, e.done(2))
                        nc.scalar.activation(kT[:, :, e.slot * P:(e.slot + 1) * P],
                                             ps[:, 6, :].rearrange("p (i n) -> p i n", n=P), ACT.Copy).then_inc(qkT_in, 1)
                    if h.there():
                        exponentials(h, 1)
                    if b.there():
                        act.wait_ge(v_done, b.done())
                        if b.back(3).there():
                            act.wait_ge(pv_done, b.back(3).done())
                        nc.scalar.activation(va[:, b.slot, :, :], ps[:, 2, :].rearrange("p (h d) -> p h d", d=DH), ACT.Copy).then_inc(v_in, 1)
                    if o.there():
                        act.wait_ge(pv_done, o.done())
                        if o.back(1).there():
                            act.wait_ge(wo_done, o.back(1).done())
                        nc.scalar.activation(oT[:, :], ps[:, 7, :], ACT.Copy).then_inc(oT_in, 1)
                    if h.there():
                        fetch_pT(h, 0)
                    if t.there():
                        act.wait_ge(xT_done, t.done())
                        c = t.slot * P
                        both = ps[:, 2, 0:2 * P].rearrange("p (a n) -> p a n", a=2)
                        nc.scalar.activation(hT[0:64, :, c:c + P].bitcast(F32R), both[0:64], ACT.Copy)
                        nc.scalar.activation(hT[64:P, :, c + 1:c + P + 1].bitcast(F32R), both[64:P], ACT.Copy).then_inc(hT_ready, 1)
                    if e.there():
                        exponentials(e, 0)
                    if h.there():
                        fetch_pT(h, 1)
                    stage(t.back(-1))
                    if t.there():
                        act.wait_ge(qk_done, t.done())
                        if t.back(1).there():
                            act.wait_ge(ss_raw, t.back(1).done())
                        nc.scalar.activation(sq[:, :].rearrange("p (a n) -> p a n", a=2), ps[:, 0:2, :], ACT.Square).then_inc(squared, 1)

                stage(Tile(l, 0, 0))
                tile_steps(act, l, 4, step)

                act.wait_ge(ffn_w_in, 16 * N_FFN_W * (l + 1))
                nc.scalar.activation(w1_hl[:, 0, :].bitcast(F32R), w1_s[:, :], ACT.Copy).then_inc(w1_hi, 1)
                act.wait_ge(x_attn, NT * (l + 1))
                load_attn(1 - l)
                act.wait_ge(norm_ready, 2 * l + 1)

                def ffn(s, n):
                    g = l * SEQS + s

                    def gelu(c):
                        r = g - 2
                        act.wait_ge(w1_done, CH * r + c + 1)
                        rows = HC if c < CH - 1 else HL
                        if c >= 2 or past(n, 3):
                            act.wait_ge(u_ready, CH * r + c - 1)
                        nc.scalar.activation(gl[0:rows, c % 2, :], ps[0:rows, 3 + 2 * (c % 2), :], ACT.Gelu,
                                             bias=b1_s[0:rows, 1, c:c + 1]).then_inc(gelu_done, 1)

                    if n == SEQS:
                        act.wait_ge(norm_ready, 2 * l + 2)
                    if on(n, 2):
                        gelu(0)
                        gelu(1)
                    if on(n, 1):
                        r = g - 1
                        if past(n, 2):
                            act.wait_ge(hnT_lo, r)
                        for part, dst, src in ((slice(64, P), slice(0, 1), norm0[64:P, bass.ds(s - 1, 1)]),
                                               (slice(0, 64), slice(0, SEQ), ps[0:64, 1, :]),
                                               (slice(64, P), slice(1, SEQ + 1), ps[64:P, 1, :])):
                            if dst.stop == SEQ:
                                act.wait_ge(hnT_done, r + 1)
                            last = nc.scalar.activation(hnT[part, dst], src, ACT.Identity,
                                                        bias=lgb_s[part, 1:2], scale=lgb_s[part, 0:1])
                        last.then_inc(hnT_in, 1)
                    if on(n, 2):
                        gelu(CH - 1)
                    if on(n, 1):
                        act.wait_ge(hnT_in, r + 1)
                        if past(n, 2):
                            act.wait_ge(w1_done, CH * r)
                        nc.scalar.activation(hnT_hl[:, 0, :].bitcast(F32R), hnT[:, 0:SEQ], ACT.Copy).then_inc(hnT_hi, 1)
                    if n == 2:
                        split_wqkv(l + 2)

                seq_steps(act, 2, ffn)

            act.wait_ge(attn_w_in, 16 * N_ATTN_W * (DEPTH + 1))
            act.wait_ge(e_nb, 1)
            with act.Fori(0, SEQS // E_GROUP) as k:
                for m in range(E_GROUP - 1):
                    for i in range(TILES):
                        t = (k * E_GROUP + m) * TILES + i
                        last = nc.scalar.activation(x1[:, t, :], x1[:, t, :], ACT.Identity, bias=e_tmp[:, 5, bass.ds(t, 1)])
                    last.then_inc(e_bias, 1)

        @block.vector
        def _(dve):
            dve.wait_ge(setup_done, SETUPS)

            places = count()

            def take_wait():
                col = next(places) % WAITS
                nc.vector.memset(waited[:, col:col + 1], 0.0)

            def spread(k, src, st_sem, s):
                take_wait()
                for i in range(TILES):
                    nc.vector.bn_stats(stats[:, k, i, :], src(i)).then_inc(st_sem, 1)
                dve.wait_ge(st_sem, TILES * (s + 1))
                take_wait()
                for i in range(TILES):
                    last = nc.vector.bn_aggr(mv[:, k, i, :], stats[:, k, i, :])
                return last

            def ret(s, n):
                if on(n, 0):
                    dve.wait_ge(x_in, 16 * (s + 1))
                    last = spread(0, lambda i: x1[:, s * TILES + i, :], x_st, s)
                if on(n, 4):
                    r = s - 4
                    dve.wait_ge(x1_ready, r + 1)
                    last = spread(2, lambda i: x1[:, r * TILES + i, :], f_st, r)
                if on(n, 3):
                    r = s - 3
                    dve.wait_ge(ret_o_done, r + 1)
                    last = spread(1, lambda i: ps[:, 7, i * P:(i + 1) * P], o_st, r)
                if on(n, 0) or on(n, 4) or on(n, 3):
                    last.then_inc(var_ready, 1)
                dve.wait_ge(std_ready, s + 1)
                if past(n, 1):
                    if n is None or n <= SEQS:
                        dve.wait_ge(xn_ready, s)
                if past(n, 5):
                    dve.wait_ge(stream, s - 4)
                nc.vector.reciprocal(rstd[:, :, :], std[:, :, :]).then_inc(rstd_ready, 1)
                dve.wait_ge(rstd_ready, s + 1)
                nc.vector.scalar_tensor_tensor(out=nbias[:, :, :], in0=mv[:, :, :, 0], scalar=-1.0, in1=rstd[:, :, :],
                                               op0=ALU.mult, op1=ALU.mult).then_inc(scal_ready, 1)
                if on(n, 2):
                    r = s - 2
                    if n == 2:
                        dve.wait_ge(consts_in, 16 * N_CONSTS)
                    dve.wait_ge(ret_s_done, r + 1)
                    if past(n, 3):
                        dve.wait_ge(ret_o_done, r)
                    for j in range(TILES):
                        w = SEQ - j * P
                        src = ps[:, 4 + j, 0:w] if j < 3 else ps[:, 6, 2 * P:3 * P]
                        last = nc.vector.tensor_tensor(sT[:, j, 0:w], src, decay_s[:, 0:w], ALU.mult)
                    last.then_inc(decayed, 1)

            seq_steps(dve, 4, ret)

            dve.wait_ge(tables_in, 16 * N_TABLES)
            nc.vector.tensor_copy(id_b[:, :], id_f[:, :]).then_inc(bf16_ready, 1)
            nc.vector.tensor_copy(mask_b[:, :], mask_f).then_inc(bf16_ready, 1)

            with dve.Fori(0, DEPTH) as l:
                dve.wait_ge(attn_w_in, 16 * N_ATTN_W * (l + 1))
                for w in range(2):
                    sc = qks_s[:, w, :].unsqueeze(1).to_broadcast([P, TILES, DH])
                    nc.vector.tensor_tensor(tab[:, :, 0, w, :], rot_s[:, :, 2 * w, :], sc, ALU.mult)
                    for a, b in ((0, 32), (32, 0)):
                        sc = qks_s[:, w, b:b + 32].unsqueeze(1).to_broadcast([P, TILES, 32])
                        last = nc.vector.tensor_tensor(tab[:, :, 1, w, a:a + 32], rot_s[:, :, 2 * w + 1, a:a + 32], sc, ALU.mult)
                last.then_inc(tab_ready, 1)
                dve.wait_ge(tab_ready, l + 1)

                def moments(part):
                    a, b = (q * TILES for q in PARTS[part])
                    own = H_STEPS * (2 * l + part)
                    dve.wait_ge(h_st, NT * l + b)
                    st, mom, df = h_stats[:, :, a:b, :], h_mom[:, :, :, a:b], h_diff[:, :, a:b]
                    nc.vector.tensor_tensor(mom[:, :, 0], st[:, :, :, 1], st[:, :, :, 4], ALU.add)
                    nc.vector.tensor_tensor(mom[:, :, 1], st[:, :, :, 2], st[:, :, :, 5], ALU.add)
                    nc.vector.tensor_tensor(df, st[:, :, :, 1], st[:, :, :, 4], ALU.subtract).then_inc(h_step, 1)
                    dve.wait_ge(h_step, own + 1)
                    nc.vector.tensor_tensor(df, df, df, ALU.mult).then_inc(h_step, 1)
                    dve.wait_ge(h_step, own + 2)
                    nc.vector.scalar_tensor_tensor(out=mom[:, :, 1], in0=df, scalar=DIM / 8.0, in1=mom[:, :, 1],
                                                   op0=ALU.mult, op1=ALU.add).then_inc(mom_ready, 1)

                def roots(part):
                    a, b = (q * TILES for q in PARTS[part])
                    own = H_STEPS * (2 * l + part)
                    total, diff, var, half, y, tmp = (e_tmp[:, i, a:b] for i in range(6))
                    dve.wait_ge(mom_ready, 2 * l + part + 1)
                    dve.wait_ge(mom_moved, 2 * l + part + 1)
                    moved = ps[:, 0, 0:2 * (b - a)].rearrange("p (a n) -> p a n", a=2)
                    nc.vector.tensor_tensor(total, h_mom[:, 0, 0, a:b], moved[:, 0, :], ALU.add)
                    nc.vector.tensor_tensor(var, h_mom[:, 0, 1, a:b], moved[:, 1, :], ALU.add)
                    nc.vector.tensor_tensor(diff, h_mom[:, 0, 0, a:b], moved[:, 0, :], ALU.subtract).then_inc(h_step, 1)
                    dve.wait_ge(h_step, own + 3)
                    nc.vector.tensor_tensor(diff, diff, diff, ALU.mult)
                    nc.vector.tensor_scalar(var, var, 1.0 / DIM, EPS, ALU.mult, ALU.add).then_inc(h_step, 1)
                    dve.wait_ge(h_step, own + 4)
                    nc.vector.scalar_tensor_tensor(out=var, in0=diff, scalar=1.0 / 16, in1=var, op0=ALU.mult,
                                                   op1=ALU.add).then_inc(h_step, 1)
                    dve.wait_ge(h_step, own + 5)
                    Newton(dve, nc, f_newt, NEWTON_STEPS * (2 * l + part), var, half, y, tmp).whole()
                    dve.wait_ge(f_newt, NEWTON_STEPS * (2 * l + part + 1))
                    nc.vector.tensor_copy(norm[:, 0, a:b, 0], y)
                    nc.vector.scalar_tensor_tensor(out=norm[:, 1, a:b, 0], in0=total, scalar=-0.25, in1=y,
                                                   op0=ALU.mult, op1=ALU.mult).then_inc(norm_own, 1)

                def neighbours(part):
                    a, b = PARTS[part]
                    count = 2 * (b - a) * TILES
                    dve.wait_ge(norm_moved, 2 * l + part + 1)
                    nc.vector.tensor_copy(norm[:, :, a * TILES:b * TILES, 1],
                                          ps[:, 0, 0:count].rearrange("p (a n) -> p a n", a=2))
                    nc.vector.tensor_copy(norm0[:, a:b], ps[:, 0, count:count + b - a]).then_inc(norm_ready, 1)

                def step(t):
                    h = t.back(3)

                    def invert(a):
                        if h.there():
                            dve.wait_ge(p_ready, 2 * h.done() - 1 + a)
                            if h.back(1).there():
                                dve.wait_ge(pn_ready, 2 * h.back(1).done() - 1 + a)
                            part = slice(a * PAIRS, (a + 1) * PAIRS)
                            nc.vector.reciprocal(rsum[:, part], psum_p[:, part]).then_inc(rsum_ready, 1)

                    def maxima(a):
                        if e.there():
                            dve.wait_ge(s_done, 2 * e.done() - 1 + a)
                            if e.back(1).there():
                                dve.wait_ge(p_ready, 2 * e.back(1).done() - 1 + a)
                            nc.vector.tensor_reduce(out=smax[:, a * PAIRS:(a + 1) * PAIRS],
                                                    in_=ps[:, 3 + a, :].rearrange("p (h c) -> p h c", c=P),
                                                    axis=AXX, op=ALU.max, negate=True).then_inc(smax_done, 1)

                    invert(0)
                    b = t.back(1)
                    e = t.back(2)
                    if b.there():
                        dve.wait_ge(squared, b.done())
                        nc.vector.tensor_reduce(out=ss[:, :], in_=sq[:, :].rearrange("p (h d) -> p h d", d=DH),
                                                axis=AXX, op=ALU.add).then_inc(ss_raw, 1)
                        if b.back(1).there():
                            dve.wait_ge(summed, b.back(1).done())
                        root = Newton(dve, nc, newt, b.back(1).done(NEWTON_STEPS), ss[:, :], nt_half[:, :], rn[:, :], nt_tmp[:, :])

                        def rotate(dst, k, w, to, frm, n):
                            return nc.vector.tensor_tensor(
                                dst[:, w, :].rearrange("p a (h d) -> p a h d", d=DH)[:, :, :, to:to + n],
                                ps[:, w, :].rearrange("p a (h d) -> p a h d", d=DH)[:, :, :, frm:frm + n],
                                tab[:, b.slot, k, w, to:to + n].unsqueeze(2).to_broadcast([P, w.stop - w.start, HEADS, n]), ALU.mult)

                        half = DH // 2
                        rotate(qk_c, 0, slice(0, 1), 0, 0, DH)
                        dve.wait_ge(ss_raw, b.done())
                        nc.vector.tensor_scalar(ss[:, :], ss[:, :], 1e-24, None, ALU.max).then_inc(ss_ready, 1)
                        rotate(qk_c, 0, slice(1, 2), 0, 0, DH)
                        dve.wait_ge(ss_ready, b.done())
                        root.seed()
                    invert(1)
                    if b.there():
                        rotate(qk_s, 1, slice(0, 2), 0, half, half)
                        if b.back(1).there():
                            dve.wait_ge(qk_ready, b.back(1).done(2))
                        root.guess()
                        rotate(qk_s, 1, slice(0, 2), half, 0, half).then_inc(rotated, 1)
                        root.square(0)
                    maxima(0)
                    if b.there():
                        root.times_v(0)
                        root.update(0)
                        for k in range(1, NEWTON):
                            root.square(k)
                            root.times_v(k)
                            root.update(k)
                    if t.at(NT + 2):
                        roots(0)
                    if t.at(NT + 3):
                        neighbours(0)
                    if not t.there():
                        maxima(1)
                    o = t.back(4)
                    if o.there():
                        dve.wait_ge(wo_done, o.done())
                        nc.vector.tensor_tensor(xf[:, o.n, :], xf[:, o.n, :], ps[:, 2, 2 * P:3 * P], ALU.add).then_inc(x_attn, 1)
                    if t.there():
                        maxima(1)
                    w = t.back(5)
                    if w.there():
                        dve.wait_ge(x_attn, w.done())
                        take_wait()
                        nc.vector.bn_stats(h_stats[:, 0, w.n, :], xf[:, w.n, 0:64])
                        nc.vector.bn_stats(h_stats[:, 1, w.n, :], xf[:, w.n, 64:P]).then_inc(h_st, 1)

                    if t.at(NT + 1):
                        moments(0)

                tile_steps(dve, l, 5, step)

                moments(1)
                dve.wait_ge(ffn_w_in, 16 * N_FFN_W * (l + 1))

                def ffn(s, n):
                    g = l * SEQS + s
                    if on(n, 2):
                        r = g - 2
                        for c in range(CH):
                            dve.wait_ge(gelu_done, CH * r + c + 1)
                            if past(n, 3):
                                dve.wait_ge(w2_done, r)
                            rows = HC if c < CH - 1 else HL
                            nc.vector.scalar_tensor_tensor(
                                out=u[0:rows, c, :], in0=ps[0:rows, 2 + 2 * (c % 2), :], scalar=b1_s[0:rows, 0, c:c + 1],
                                in1=gl[0:rows, c % 2, :], op0=ALU.add, op1=ALU.mult).then_inc(u_ready, 1)
                    if on(n, 1):
                        dve.wait_ge(hnT_hi, g)
                        nc.vector.tensor_tensor(hnT_hl[:, 1, :].bitcast(F32R), hnT[:, 0:SEQ], hnT_hl[:, 0, :],
                                                ALU.subtract).then_inc(hnT_lo, 1)
                    if n == 1:
                        roots(1)
                    if on(n, 3):
                        dve.wait_ge(stream, SEQS + g - 2)
                        take_wait()
                        for i in range(TILES):
                            last = nc.vector.bn_stats(e_stats[:, (s - 3) * TILES + i, :], xf[:, (s - 3) * TILES + i, :])
                        last.then_inc(e_st, 1)
                    if on(n, 2):
                        r = g - 2
                        dve.wait_ge(w2_done, r + 1)
                        nc.vector.tensor_tensor(seq_rows(xf, s - 2), seq_rows(xf, s - 2),
                                                ps[:, 6, :].rearrange("p (t d) -> p t d", t=TILES), ALU.add).then_inc(stream, 1)

                    if n == 2:
                        neighbours(1)

                seq_steps(dve, 3, ffn)

            dve.wait_ge(e_st, SEQS * DEPTH)
            m_even, m_odd = e_stats[:, :, 1], e_stats[:, :, 4]
            total, diff, var, half, y, nb = (e_tmp[:, i, :] for i in range(6))
            nc.vector.tensor_tensor(total, m_even, m_odd, ALU.add)
            nc.vector.tensor_tensor(var, e_stats[:, :, 2], e_stats[:, :, 5], ALU.add)
            nc.vector.tensor_tensor(diff, m_even, m_odd, ALU.subtract).then_inc(e_st, 1)
            dve.wait_ge(e_st, SEQS * DEPTH + 1)
            nc.vector.tensor_tensor(diff, diff, diff, ALU.mult)
            nc.vector.tensor_scalar(var, var, 1.0 / DIM, EPS, ALU.mult, ALU.add).then_inc(e_st, 1)
            dve.wait_ge(e_st, SEQS * DEPTH + 2)
            nc.vector.scalar_tensor_tensor(out=var, in0=diff, scalar=0.25, in1=var, op0=ALU.mult, op1=ALU.add).then_inc(e_st, 1)
            dve.wait_ge(e_st, SEQS * DEPTH + 3)
            Newton(dve, nc, e_newt, 0, var, half, y, diff).whole()
            dve.wait_ge(e_newt, NEWTON_STEPS)
            nc.vector.scalar_tensor_tensor(out=nb, in0=total, scalar=-0.5, in1=y, op0=ALU.mult, op1=ALU.mult).then_inc(e_nb, 1)
            with dve.Fori(0, SEQS // E_GROUP) as k:
                for m in range(E_GROUP - 1):
                    dve.wait_ge(e_bias, k * (E_GROUP - 1) + m + 1)
                    for i in range(TILES):
                        t = (k * E_GROUP + m) * TILES + i
                        last = nc.vector.scalar_tensor_tensor(out=x1[:, t, :], in0=xf[:, t, :], scalar=e_tmp[:, 4, bass.ds(t, 1)],
                                                              in1=x1[:, t, :], op0=ALU.mult, op1=ALU.add)
                    last.then_inc(e_sum, 1)

        @block.tensor
        def _(pe):
            pe.wait_ge(setup_done, SETUPS)
            pe.wait_ge(consts_in, 16 * N_CONSTS)
            pe.wait_ge(ret_w_in, 16 * N_RET_W)
            mm = nc.tensor.matmul

            def ret(s, n):
                if on(n, 2):
                    r = s - 2
                    pe.wait_ge(xnT_in, r + 1)
                    if past(n, 3):
                        pe.wait_ge(rqk_in, r)
                        pe.wait_ge(rv_in, r)
                    mm(ps[:, 1, :], wq_s[:, :], xnT[:, :], start=True, stop=True).then_inc(proj_done, 1)
                    mm(ps[:, 2, :], wk_s[:, :], xnT[:, :], start=True, stop=True).then_inc(proj_done, 1)
                    for i in range(TILES):
                        last = mm(ps[:, 3, i * P:(i + 1) * P], xnT[:, i * P:(i + 1) * P], wv_s[:, :], start=True, stop=True)
                    last.then_inc(proj_done, 1)
                if on(n, 3):
                    r = s - 3
                    pe.wait_ge(decayed, r + 1)
                    pe.wait_ge(rv_in, r + 1)
                    if past(n, 4):
                        pe.wait_ge(on_ready, r)
                    for i in range(TILES):
                        for j in range(i + 1):
                            last = mm(ps[:, 7, i * P:(i + 1) * P], sT[:, j, (i - j) * P:(i - j + 1) * P],
                                      rv[:, j * P:(j + 1) * P], start=(j == 0), stop=(j == i))
                    last.then_inc(ret_o_done, 1)
                if on(n, 1):
                    r = s - 1
                    pe.wait_ge(xn_ready, r + 1)
                    if past(n, 2):
                        pe.wait_ge(xnT_in, r)
                    for i in range(TILES):
                        last = nc.tensor.transpose(ps[:, 0, i * P:(i + 1) * P], xn[:, i, :], id_f[:, :])
                    last.then_inc(xnT_done, 1)
                if on(n, 2):
                    r = s - 2
                    pe.wait_ge(rqk_in, r + 1)
                    if past(n, 3):
                        pe.wait_ge(decayed, r)
                    for j in range(TILES):
                        w = SEQ - j * P
                        dst = ps[:, 4 + j, 0:w] if j < 3 else ps[:, 6, 2 * P:3 * P]
                        last = mm(dst, rk[:, j * P:(j + 1) * P], rq[:, j * P:SEQ], start=True, stop=True)
                    last.then_inc(ret_s_done, 1)

            seq_steps(pe, 4, ret)

            pe.wait_ge(tables_in, 16 * N_TABLES)
            pe.wait_ge(bf16_ready, 2)
            with pe.Fori(0, DEPTH) as l:
                pe.wait_ge(stream, SEQS * (l + 1) - 1)
                pe.wait_ge(attn_w_in, 16 * N_ATTN_W * (l + 1))
                pe.wait_ge(wqkv_lo, l + 1)

                def shifted(part, src, kinds, to_next):
                    a, b = PARTS[part]
                    count = kinds * (b - a) * TILES
                    slots = slice(0, TILES - 1), slice(1, TILES)
                    frm, to = slots if to_next else slots[::-1]
                    m = 0 if to_next else 2
                    mm(ps[:, 0, 0:count], shift_s[:, m, :], src, start=True, stop=False, skip_group_check=True)
                    for kind in range(kinds):
                        span = (b - a) * TILES
                        last = mm(ps[:, 0, kind * span:(kind + 1) * span].rearrange("p (s t) -> p s t", t=TILES)[:, :, to],
                                  shift_s[:, m + 1, :], src[:, kind].rearrange("p (s t) -> p s t", t=TILES)[:, :, frm],
                                  start=False, stop=True, skip_group_check=True)
                    return last

                def move_moments(part):
                    a, b = (q * TILES for q in PARTS[part])
                    pe.wait_ge(mom_ready, 2 * l + part + 1)
                    if part:
                        pe.wait_ge(norm_ready, 2 * l + part)
                    else:
                        pe.wait_ge(rotated, NT * (l + 1))
                    shifted(part, h_mom[:, 1, :, a:b], 2, True).then_inc(mom_moved, 1)

                def move_scalars(part):
                    a, b = PARTS[part]
                    pe.wait_ge(norm_own, 2 * l + part + 1)
                    shifted(part, norm[:, :, a * TILES:b * TILES, 0], 2, False)
                    count = 2 * (b - a) * TILES
                    mm(ps[:, 0, count:count + b - a], shift_s[:, 4, :],
                       norm[:, 1, a * TILES:b * TILES, 0].rearrange("p (s t) -> p s t", t=TILES)[:, :, 0],
                       start=True, stop=True).then_inc(norm_moved, 1)

                def step(t):
                    d, b, h, o = t.back(2), t.back(1), t.back(3), t.back(4)
                    if b.there():
                        pe.wait_ge(hT_ready, b.done())
                        if b.back(1).there():
                            pe.wait_ge(rotated, b.back(1).done())
                            pe.wait_ge(squared, b.back(1).done())
                        c = b.slot * P
                        for banks, done in (((0, 1), qk_done), ((2,), v_done)):
                            if banks == (2,) and b.back(4).there():
                                pe.wait_ge(x_attn, b.back(4).done())
                            for x_part, w_part in ((0, 0), (0, 1), (1, 0)):
                                for w in banks:
                                    last = mm(ps[:, w, :], hT[:, x_part, c:c + P].bitcast(F32R),
                                              wqkv_hl[:, w_part, w * INNER:(w + 1) * INNER].bitcast(F32R),
                                              start=(x_part + w_part == 0), stop=(x_part == 1))
                            last.then_inc(done, 1)
                    if t.at(2):
                        pe.wait_ge(stream, SEQS * (l + 1))
                    if d.there():
                        for w in range(2):
                            pe.wait_ge(qk_ready, 2 * d.done() - 1 + w)
                            if d.back(2).there():
                                pe.wait_ge(pT_in, 2 * d.back(2).done() - 1 + w)
                            for i in range(PAIRS):
                                last = nc.tensor.transpose(ps[:, 5 + w, i * P:(i + 1) * P], qk[:, w, i * P:(i + 1) * P], id_f[:, :])
                            last.then_inc(qkT_done, 1)
                    if o.there():
                        pe.wait_ge(pT_in, o.done(2))
                        pe.wait_ge(vb_in[o.slot], (16 if o.slot == 0 else 32) * (o.layer * SEQS + o.batch + 1))
                        if o.back(1).there():
                            pe.wait_ge(oT_in, o.back(1).done())
                        for i in range(HEADS):
                            j, par = i % 2 * PAIRS + i // 2, i % 2
                            for half, values in enumerate((vb, va)):
                                q = slice(half * WIN, (half + 1) * WIN)
                                last = mm(ps[par * DH:(par + 1) * DH, 7, i // 2 * P + q.start:i // 2 * P + q.stop],
                                          values[:, o.slot, i, :], pT[:, j, q], start=True, stop=True)
                        last.then_inc(pv_done, 1)
                    if t.at(NT + 2):
                        move_moments(0)
                    if t.at(NT + 3):
                        move_scalars(0)

                    def transpose_p(a):
                        if h.there():
                            if d.there():
                                pe.wait_ge(qkT_in, 2 * d.done() - 1 + a)
                            pe.wait_ge(pn_ready, 2 * h.done() - 1 + a)
                            for i in range(PAIRS):
                                last = nc.tensor.transpose(ps[:, 5 + a, i * P:(i + 1) * P], prob[:, a * PAIRS + i, :], id_f[:, :])
                            last.then_inc(pT_done, 1)

                    def scores(par):
                        if d.there():
                            if par == 0:
                                pe.wait_ge(qkT_in, d.done(2))
                            if d.back(1).there():
                                pe.wait_ge(p_ready, 2 * d.back(1).done() - 1 + par)
                            v = 1 if d.slot else 0
                            mm(ps[:, 3 + par, :], id_b[:, :], mask_b[:, v * 512:(v + 1) * 512], start=True, stop=False,
                               skip_group_check=True)
                            r = slice(par * DH, (par + 1) * DH)
                            for i in range(PAIRS):
                                for half in range(2):
                                    first = d.slot == 0 and half == 0
                                    lo = d.slot * P + (0 if first else (half - 1) * WIN)
                                    hi = d.slot * P + (half + 1) * WIN
                                    last = mm(ps[half * WIN:(half + 1) * WIN, 3 + par, (i + 1) * P - (hi - lo):(i + 1) * P],
                                              qT[r, i * P + half * WIN:i * P + (half + 1) * WIN], kT[r, i, lo:hi],
                                              start=False, stop=(i == PAIRS - 1), skip_group_check=True)
                            last.then_inc(s_done, 1)

                    transpose_p(0)
                    scores(0)
                    if t.there():
                        pe.wait_ge(x_lo, t.done())
                        if t.back(1).there():
                            pe.wait_ge(v_in, t.back(1).done())
                        nc.tensor.transpose(ps[:, 2, 0:P], xstage[:, t.slot % 2, 0, :], id_f[:, :])
                        nc.tensor.transpose(ps[:, 2, P:2 * P], xstage[:, t.slot % 2, 1, :], id_f[:, :]).then_inc(xT_done, 1)
                    scores(1)
                    transpose_p(1)
                    if o.there():
                        pe.wait_ge(oT_in, o.done())
                        if t.there():
                            pe.wait_ge(hT_ready, t.done())
                        elif b.there():
                            pe.wait_ge(v_in, b.done())
                        if o.back(1).there():
                            pe.wait_ge(x_attn, o.back(1).done())
                        for i in range(PAIRS):
                            last = mm(ps[:, 2, 2 * P:3 * P], oT[:, i * P:(i + 1) * P], wo_s[:, i, :], start=(i == 0), stop=(i == PAIRS - 1))
                        last.then_inc(wo_done, 1)


                tile_steps(pe, l, 4, step)


                def ffn(s, n):
                    g = l * SEQS + s

                    def w1_product(c):
                        r = g - 2
                        rows = HC if c < CH - 1 else HL
                        if c == 0:
                            pe.wait_ge(hnT_lo, r + 1)
                        if c >= 2 or past(n, 3):
                            pe.wait_ge(u_ready, CH * r + c - 1)
                        for h in range(2):
                            cols = slice(h * HID + c * HC, h * HID + c * HC + rows)
                            for w_part, x_part in ((0, 0), (0, 1), (1, 0)):
                                last = mm(ps[0:rows, 2 + 2 * (c % 2) + h, :], w1_hl[:, w_part, cols].bitcast(F32R),
                                          hnT_hl[:, x_part, :].bitcast(F32R), start=(w_part + x_part == 0), stop=(w_part == 1))
                        last.then_inc(w1_done, 1)

                    if n == 2:
                        pe.wait_ge(w1_lo, l + 1)
                        pe.wait_ge(ffn_w_in, 16 * N_FFN_W * (l + 1))
                    if on(n, 2):
                        w1_product(0)
                        w1_product(1)
                    if on(n, 1):
                        r = g - 1
                        pe.wait_ge(hn_ready, r + 1)
                        if past(n, 2):
                            pe.wait_ge(hnT_in, r)
                        for i in range(TILES):
                            last = nc.tensor.transpose(ps[:, 1, i * P:(i + 1) * P], hn[:, i, :], id_f[:, :])
                        last.then_inc(hnT_done, 1)
                    if n == 1:
                        move_moments(1)
                    if on(n, 2):
                        w1_product(2)
                        r = g - 2
                        if past(n, 3):
                            pe.wait_ge(stream, SEQS + r)
                        for c in range(CH):
                            pe.wait_ge(u_ready, CH * r + c + 1)
                            for i in range(TILES):
                                last = mm(ps[:, 6, i * P:(i + 1) * P], u[0:HC, c, i * P:(i + 1) * P], w2_s[:, c, :],
                                          start=(c == 0 and i == 0), stop=(c == CH - 1), skip_group_check=True)
                        last.then_inc(w2_done, 1)
                    if n == 2:
                        move_scalars(1)

                seq_steps(pe, 2, ffn)


def kernel(L0_attn_x, L0_attn_Wq, L0_attn_bq, L0_attn_Wk, L0_attn_bk, L0_attn_Wv, L0_ffn_wqkv, L0_ffn_q_scale,
           L0_ffn_k_scale, L0_ffn_wo, L0_ffn_ln_g, L0_ffn_ln_b, L0_ffn_w1, L0_ffn_b1, L0_ffn_w2, L0_ffn_b2):
    import concourse.bacc as bacc
    from concourse.bass_utils import run_bass_kernel_spmd

    a = np.asarray
    b1 = np.zeros((DEPTH, 2, CH * HC), np.float32)
    b1[:, :, 0:HID] = a(L0_ffn_b1).reshape(DEPTH, 2, HID)
    w2 = np.concatenate([a(L0_ffn_w2), a(L0_ffn_b2)[:, None, :]], axis=1)
    qks = np.stack([a(L0_ffn_q_scale), a(L0_ffn_k_scale)], axis=1)
    arrays = {
        "x": a(L0_attn_x).reshape(SEQS * SEQ, DIM),
        "wq": a(L0_attn_Wq).T, "wk": a(L0_attn_Wk).T, "wv": a(L0_attn_Wv).T,
        "bqk": np.stack([a(L0_attn_bq), a(L0_attn_bk)], axis=1),
        "wqkv": a(L0_ffn_wqkv),
        "qks": np.broadcast_to(qks[:, None], (DEPTH, P, 2, DH)),
        "wo": a(L0_ffn_wo),
        "lgb": np.stack([a(L0_ffn_ln_g), a(L0_ffn_ln_b)], axis=2),
        "w1": a(L0_ffn_w1),
        "b1": b1.reshape(DEPTH, 2, CH, HC).transpose(0, 3, 1, 2),
        "w2": w2.reshape(DEPTH, CH, HC, P).transpose(0, 2, 1, 3),
        **shape_constants(),
    }
    nc = bacc.Bacc("TRN2", target_bir_lowering=False, num_devices=1)
    args, sent = [], {}
    for name, v in arrays.items():
        v = np.ascontiguousarray(v)
        sent[f"in_{name}_dram"] = v
        args.append(nc.dram_tensor(f"in_{name}_dram", v.shape, mybir.dt.from_np(v.dtype), kind="ExternalInput").ap())
    args.append(nc.dram_tensor("out_0_dram", (SEQS * SEQ, DIM), F32, kind="ExternalOutput").ap())
    build(nc, *args)
    r = run_bass_kernel_spmd(nc, [sent], core_ids=[0])
    return r.results[0]["out_0_dram"].reshape(SEQS, SEQ, DIM)
```
